# Optimizing a Trainium2 kernel written in Bass

```python
import numpy as np
import jax
import jax.numpy as jnp

def _softmax(x, axis=-1):
    return jax.nn.softmax(x, axis=axis)
def _gelu(x):
    return jax.nn.gelu(x, approximate=True)
def _silu(x):
    return jax.nn.silu(x)
def _sigmoid(x):
    return jax.nn.sigmoid(x)
def _layernorm(x, axis=-1, eps=1e-5):
    m = jnp.mean(x, axis=axis, keepdims=True)
    v = jnp.var(x, axis=axis, keepdims=True)
    return (x - m) / jnp.sqrt(v + eps)
def _scatter_add(tgt, idx, src, axis=0):
    return tgt.at[idx].add(src)
def _segment_sum(src, seg, n):
    return jax.ops.segment_sum(src, seg, n)

kernel_name = 'mk_conv_preact_d2_conv_nhwc192_42a537'

def setup_inputs(seed: int = 0):
    np.random.seed(seed)
    _w = jnp.asarray
    def _rec_inputs():
        import jax
        import jax.numpy as jnp
        _gk = jax.random.key(seed)
        x = 0.0002141 + 1 * jax.random.normal(jax.random.fold_in(_gk, 1), (4, 32, 32, 192), jnp.float32)
        return x
    x = _rec_inputs()
    def _L0_conv_setup():
        import jax, jax.numpy as jnp
        import numpy as np
        D_MODEL = 192
        D_STATE = 16
        D_CONV = 3
        EXPAND = 2
        D_INNER = EXPAND * D_MODEL
        DT_RANK = (D_MODEL + 15) // 16

        def _ssm_scan(u, W_x, W_dt, b_dt, A_log, D_param):
            x_dbl = u @ W_x
            dt = x_dbl[..., :DT_RANK]
            B_mat = x_dbl[..., DT_RANK:DT_RANK + D_STATE]
            C_mat = x_dbl[..., DT_RANK + D_STATE:]
            dt = jax.nn.softplus(dt @ W_dt + b_dt)
            A = -jnp.exp(A_log)
            log_dA = jnp.einsum('bld,dn->bldn', dt, A)
            dB_u = jnp.einsum('bld,bln->bldn', dt, B_mat) * u[..., None]
            log_decay = jnp.cumsum(log_dA, axis=1)
            decay = jnp.exp(log_decay)
            h = decay * jnp.cumsum(dB_u / (decay + 1e-12), axis=1)
            y = jnp.einsum('bldn,bln->bld', h, C_mat)
            return y + u * D_param
        key = jax.random.key(seed)
        ks = jax.random.split(key, 8)
        B, H, W = (4, 32, 32)
        sc = lambda n: 1.0 / np.sqrt(n)
        x = jax.random.normal(ks[0], (B, H, W, D_MODEL), jnp.float32)
        W_in = jax.random.normal(ks[1], (D_MODEL, 2 * D_INNER), jnp.float32) * sc(D_MODEL)
        conv_w = jax.random.normal(ks[2], (D_INNER, 1, D_CONV, D_CONV), jnp.float32) * sc(D_CONV * D_CONV)
        conv_b = jnp.zeros((D_INNER,), jnp.float32)
        W_x = jax.random.normal(ks[3], (D_INNER, DT_RANK + 2 * D_STATE), jnp.float32) * sc(D_INNER)
        W_dt = jax.random.normal(ks[4], (DT_RANK, D_INNER), jnp.float32) * sc(DT_RANK)
        b_dt = jnp.zeros((D_INNER,), jnp.float32)
        A_log = jnp.log(jnp.tile(jnp.arange(1, D_STATE + 1, dtype=jnp.float32), (D_INNER, 1)))
        D_param = jnp.ones((D_INNER,), jnp.float32)
        W_out = jax.random.normal(ks[5], (D_INNER, D_MODEL), jnp.float32) * sc(D_INNER)
        gamma = jnp.ones((D_INNER,), jnp.float32)
        beta = jnp.zeros((D_INNER,), jnp.float32)
        return {'x': x, 'W_in': W_in, 'conv_w': conv_w, 'conv_b': conv_b, 'W_x': W_x, 'W_dt': W_dt, 'b_dt': b_dt, 'A_log': A_log, 'D_param': D_param, 'W_out': W_out, 'gamma': gamma, 'beta': beta}
    _L0_conv_all = _L0_conv_setup()
    _L0_conv_in = {k: v for k, v in _L0_conv_all.items() if k in ('W_in', 'conv_w', 'conv_b', 'W_x', 'W_dt', 'b_dt', 'A_log', 'D_param', 'W_out', 'gamma', 'beta', )}
    del _L0_conv_all

    def _L1_conv_setup():
        import jax, jax.numpy as jnp
        import numpy as np
        DECAY = 0.6
        GAIN = 0.4
        LN_EPS = 1e-05

        def ema_scan(x, axis):
            xm = jnp.moveaxis(x, axis, 0)

            def step(s, xt):
                s = DECAY * s + GAIN * xt
                return (s, s)
            _, ys = jax.lax.scan(step, jnp.zeros_like(xm[0]), xm)
            return jnp.moveaxis(ys, 0, axis)
        key = jax.random.key(seed)
        ks = jax.random.split(key, 8)
        B, H, W, D = (8, 96, 96, 192)
        C = 2 * D
        s_in = 1.0 / np.sqrt(D)
        s_out = 1.0 / np.sqrt(C)
        return {'x': jax.random.normal(ks[0], (B, H, W, D), dtype=jnp.float32), 'W_in': jax.random.uniform(ks[1], (D, C), minval=-s_in, maxval=s_in, dtype=jnp.float32), 'b_in': jax.random.uniform(ks[2], (C,), minval=-s_in, maxval=s_in, dtype=jnp.float32), 'conv_w': jax.random.uniform(ks[3], (C, 1, 3, 3), minval=-1.0 / 3.0, maxval=1.0 / 3.0, dtype=jnp.float32), 'ln_g': jnp.ones((C,), dtype=jnp.float32), 'ln_b': jnp.zeros((C,), dtype=jnp.float32), 'W_out': jax.random.uniform(ks[4], (C, D), minval=-s_out, maxval=s_out, dtype=jnp.float32), 'b_out': jax.random.uniform(ks[5], (D,), minval=-s_out, maxval=s_out, dtype=jnp.float32)}
    _L1_conv_all = _L1_conv_setup()
    _L1_conv_in = {k: v for k, v in _L1_conv_all.items() if k in ('W_in', 'b_in', 'conv_w', 'ln_g', 'ln_b', 'W_out', 'b_out', )}
    del _L1_conv_all

    return {
        "x": x,
        "L0_conv_W_in": _L0_conv_in["W_in"],
        "L0_conv_conv_w": _L0_conv_in["conv_w"],
        "L0_conv_conv_b": _L0_conv_in["conv_b"],
        "L0_conv_W_x": _L0_conv_in["W_x"],
        "L0_conv_W_dt": _L0_conv_in["W_dt"],
        "L0_conv_b_dt": _L0_conv_in["b_dt"],
        "L0_conv_A_log": _L0_conv_in["A_log"],
        "L0_conv_D_param": _L0_conv_in["D_param"],
        "L0_conv_W_out": _L0_conv_in["W_out"],
        "L0_conv_gamma": _L0_conv_in["gamma"],
        "L0_conv_beta": _L0_conv_in["beta"],
        "L1_conv_W_in": _L1_conv_in["W_in"],
        "L1_conv_b_in": _L1_conv_in["b_in"],
        "L1_conv_conv_w": _L1_conv_in["conv_w"],
        "L1_conv_ln_g": _L1_conv_in["ln_g"],
        "L1_conv_ln_b": _L1_conv_in["ln_b"],
        "L1_conv_W_out": _L1_conv_in["W_out"],
        "L1_conv_b_out": _L1_conv_in["b_out"],
    }

def reference(x, L0_conv_W_in, L0_conv_conv_w, L0_conv_conv_b, L0_conv_W_x, L0_conv_W_dt, L0_conv_b_dt, L0_conv_A_log, L0_conv_D_param, L0_conv_W_out, L0_conv_gamma, L0_conv_beta, L1_conv_W_in, L1_conv_b_in, L1_conv_conv_w, L1_conv_ln_g, L1_conv_ln_b, L1_conv_W_out, L1_conv_b_out):
    import jax
    import jax.numpy as jnp
    def _L0_conv_ref(x, W_in, conv_w, conv_b, W_x, W_dt, b_dt, A_log, D_param, W_out, gamma, beta):
        import jax, jax.numpy as jnp
        import numpy as np
        D_MODEL = 192
        D_STATE = 16
        D_CONV = 3
        EXPAND = 2
        D_INNER = EXPAND * D_MODEL
        DT_RANK = (D_MODEL + 15) // 16

        def _ssm_scan(u, W_x, W_dt, b_dt, A_log, D_param):
            x_dbl = u @ W_x
            dt = x_dbl[..., :DT_RANK]
            B_mat = x_dbl[..., DT_RANK:DT_RANK + D_STATE]
            C_mat = x_dbl[..., DT_RANK + D_STATE:]
            dt = jax.nn.softplus(dt @ W_dt + b_dt)
            A = -jnp.exp(A_log)
            log_dA = jnp.einsum('bld,dn->bldn', dt, A)
            dB_u = jnp.einsum('bld,bln->bldn', dt, B_mat) * u[..., None]
            log_decay = jnp.cumsum(log_dA, axis=1)
            decay = jnp.exp(log_decay)
            h = decay * jnp.cumsum(dB_u / (decay + 1e-12), axis=1)
            y = jnp.einsum('bldn,bln->bld', h, C_mat)
            return y + u * D_param
        B, H, W, C = x.shape
        xz = x @ W_in
        x_val, z = (xz[..., :D_INNER], xz[..., D_INNER:])
        xc = jnp.transpose(x_val, (0, 3, 1, 2))
        xc = jax.lax.conv_general_dilated(xc, conv_w, window_strides=(1, 1), padding='SAME', feature_group_count=D_INNER, dimension_numbers=('NCHW', 'OIHW', 'NCHW'))
        xc = xc + conv_b[None, :, None, None]
        xc = jax.nn.silu(xc)
        xv = jnp.transpose(xc, (0, 2, 3, 1))
        scan = lambda u: _ssm_scan(u, W_x, W_dt, b_dt, A_log, D_param)
        s1 = xv.reshape(B, H * W, D_INNER)
        s2 = s1[:, ::-1]
        s3 = jnp.transpose(xv, (0, 2, 1, 3)).reshape(B, W * H, D_INNER)
        s4 = s3[:, ::-1]
        y1 = scan(s1)
        y2 = scan(s2)[:, ::-1]
        y3 = scan(s3)
        y4 = scan(s4)[:, ::-1]
        y3 = jnp.transpose(y3.reshape(B, W, H, D_INNER), (0, 2, 1, 3)).reshape(B, H * W, D_INNER)
        y4 = jnp.transpose(y4.reshape(B, W, H, D_INNER), (0, 2, 1, 3)).reshape(B, H * W, D_INNER)
        y = y1 + y2 + y3 + y4
        mu = jnp.mean(y, axis=-1, keepdims=True)
        var = jnp.mean(jnp.square(y - mu), axis=-1, keepdims=True)
        y = (y - mu) * jax.lax.rsqrt(var + 1e-05) * gamma + beta
        y = y.reshape(B, H, W, D_INNER) * jax.nn.silu(z)
        return y @ W_out

    def _L1_conv_ref(x, W_in, b_in, conv_w, ln_g, ln_b, W_out, b_out):
        import jax, jax.numpy as jnp
        import numpy as np
        DECAY = 0.6
        GAIN = 0.4
        LN_EPS = 1e-05

        def ema_scan(x, axis):
            xm = jnp.moveaxis(x, axis, 0)

            def step(s, xt):
                s = DECAY * s + GAIN * xt
                return (s, s)
            _, ys = jax.lax.scan(step, jnp.zeros_like(xm[0]), xm)
            return jnp.moveaxis(ys, 0, axis)
        C = W_in.shape[1]
        proj = jnp.einsum('bhwd,dc->bhwc', x, W_in) + b_in
        cf = jnp.transpose(proj, (0, 3, 1, 2))
        local = jax.lax.conv_general_dilated(cf, conv_w, window_strides=(1, 1), padding='SAME', feature_group_count=C, dimension_numbers=('NCHW', 'OIHW', 'NCHW'))
        lr = ema_scan(local, 3)
        rl = jnp.flip(ema_scan(jnp.flip(local, 3), 3), 3)
        tb = ema_scan(local, 2)
        bt = jnp.flip(ema_scan(jnp.flip(local, 2), 2), 2)
        mixed = 0.25 * (lr + rl + tb + bt) + local
        mixed = jnp.transpose(mixed, (0, 2, 3, 1))
        mu = jnp.mean(mixed, axis=-1, keepdims=True)
        var = jnp.mean(jnp.square(mixed - mu), axis=-1, keepdims=True)
        normed = (mixed - mu) * jax.lax.rsqrt(var + LN_EPS) * ln_g + ln_b
        return jnp.einsum('bhwc,cd->bhwd', normed, W_out) + b_out

    def _gn(v, G=32, eps=1e-5):
        B_, H_, W_, C_ = v.shape
        g = v.reshape(B_, H_, W_, G, C_ // G)
        m = jnp.mean(g, axis=(1, 2, 4), keepdims=True)
        s = jnp.var(g, axis=(1, 2, 4), keepdims=True)
        return ((g - m) / jnp.sqrt(s + eps)).reshape(v.shape)

    def _ln_c(v, eps=1e-6):
        m = jnp.mean(v, axis=-1, keepdims=True)
        s = jnp.var(v, axis=-1, keepdims=True)
        return (v - m) / jnp.sqrt(s + eps)

    def _ln_t(v, eps=1e-5):
        m = jnp.mean(v, axis=-1, keepdims=True)
        s = jnp.var(v, axis=-1, keepdims=True)
        return (v - m) / jnp.sqrt(s + eps)

    def _to_tokens(v):
        B_, H_, W_, C_ = v.shape
        return v.reshape(B_, H_ * W_, C_)
    def _from_tokens(t, like):
        return t.reshape(like.shape)

    x = x + _L0_conv_ref(_gn(x), L0_conv_W_in, L0_conv_conv_w, L0_conv_conv_b, L0_conv_W_x, L0_conv_W_dt, L0_conv_b_dt, L0_conv_A_log, L0_conv_D_param, L0_conv_W_out, L0_conv_gamma, L0_conv_beta)
    x = x + _L1_conv_ref(_gn(x), L1_conv_W_in, L1_conv_b_in, L1_conv_conv_w, L1_conv_ln_g, L1_conv_ln_b, L1_conv_W_out, L1_conv_b_out)
    return x


_drawn_inputs = setup_inputs


def setup_inputs(seed=0):
    import zlib

    import numpy as np

    out = dict(_drawn_inputs(seed))
    spreads = {'L0_conv_conv_b': (0.0, 0.1),
     'L0_conv_b_dt': (0.0, 0.8),
     'L0_conv_D_param': (1.0, 0.2),
     'L0_conv_gamma': (1.0, 0.2),
     'L0_conv_beta': (0.0, 0.1),
     'L1_conv_ln_g': (1.0, 0.2),
     'L1_conv_ln_b': (0.0, 0.1)}
    factors = {'L0_conv_W_x': 6.363, 'L0_conv_W_dt': 8.0, 'L0_conv_A_log': 8.0}
    for name, (base, spread) in spreads.items():
        noise = np.random.default_rng([zlib.crc32(name.encode()), seed]).standard_normal(out[name].shape)
        drawn = base * np.exp(spread * noise) if base else spread * noise
        out[name] = jnp.asarray(drawn.astype(out[name].dtype))
    for name, factor in factors.items():
        out[name] = (out[name] * factor).astype(out[name].dtype)
    return out
```

```python
from contextlib import ExitStack

import concourse.bass as bass
from concourse import mybir

F32 = mybir.dt.float32
I32 = mybir.dt.int32
ALU = mybir.AluOpType
ACT = mybir.ActivationFunctionType
AX = mybir.AxisListType

NB, HH, WW, DM = 4, 32, 32, 192
DI, NS, RK = 384, 16, 12
PX = HH * WW
NPOS = NB * PX
P = 128
CT = DI // P
MP, MT = 96, DM // 96
NX = 512
HP, WP = HH + 2, WW + 2
XD = RK + 2 * NS
GN_EPS, LN_EPS = 1e-5, 1e-5
DECAY, GAIN = 0.6, 0.4
TC = 32
NDIR = 4
SEG = NDIR * NB
SW = TC + 2
FORWARD, BY_ROW = (0, 1), (0, 2)
SETUP = 7
GUARD = 1e-12
HALF_LOG_GUARD = 13.815510557964274
CHUNK_GROUP = 4
DEAD = -104.0


class Names:
    pass


INNER = {"conv_w0": CT * 9, "conv_w1": CT * 9, "w_x": CT * XD, "a_log": CT * NS, "w_out0": CT * DM, "w_out1": CT * DM,
         "conv_b0": CT, "b_dt": CT, "d_skip": CT, "gamma0": CT, "beta0": CT, "b_in1": CT, "gamma1": CT, "beta1": CT,
         "ident": P}
MODEL = {"w_in0": MT * 2 * DI, "w_in1": MT * DI, "b_out1": MT, "group_avg": MP}


def unpack(packed, columns):
    parts, at = {}, 0
    for name, n in columns.items():
        tiles = 1 if name in ("ident", "group_avg") else CT if columns is INNER else MT
        part = packed[:, at:at + n]
        parts[name] = part if tiles == 1 or n == tiles else part.rearrange("p (t n) -> p t n", t=tiles)
        at += n
    return parts


def load(nc, t, sems, d):
    with nc.Block() as block:

        @block.sync
        def _(sp):
            for b in range(NB):
                sp.dma_start(t.x[:, :, b, :], d["x"].rearrange("(k p) (b n) -> p k b n", p=MP, b=NB)[:, :, b, :]
                             ).then_inc(sems.x_in[b], 16)
            for b in range(NB):
                sp.wait_ge(sems.x_in[b], 16)

        @block.scalar
        def _(act):
            act.dma_start(t.model_params[:, :], d["model_params"]).then_inc(sems.params, 16)
            act.dma_start(t.inner_params[:, :], d["inner_params"]).then_inc(sems.params, 16)
            act.dma_start(t.w_dt[:, :], d["w_dt"]).then_inc(sems.params, 16)
            act.wait_ge(sems.params, 16 * 3)

        @block.gpsimd
        def _(pool):
            pool.memset(t.avg_inner[:, :], 1.0 / DI).then_inc(sems.fills, 1)
            pool.memset(t.gn_eps[:, :], GN_EPS).then_inc(sems.fills, 1)
            pool.memset(t.half_log_guard[:, :], HALF_LOG_GUARD).then_inc(sems.fills, 1)
            pool.wait_ge(sems.params, 16 * 3)
            pool.tensor_scalar(t.conv_w1, t.conv_w1, GAIN / 4 * (1 - DECAY ** 2), 1.0, ALU.mult, ALU.mult).then_inc(sems.fills, 1)
            pool.wait_ge(sems.fills, 4)


def group_norm(nc, t, name, src, dst):
    with ExitStack() as ctx:
        sem = lambda what: ctx.enter_context(nc.semaphore(f"{name}_{what}"))
        sb = lambda what, shape: ctx.enter_context(nc.sbuf_tensor(f"{name}_{what}", shape, F32))
        stats = sb("stats", [MP, MT, NB, PX // NX, 6])
        channel = sb("channel", [MP, MT, NB, 2])
        spread = sb("spread", [MP, MT, NB])
        std = sb("std", [MP, MT, NB])
        group_mean = ctx.enter_context(nc.psum_tensor(f"{name}_gm", [MP, MT, NB], F32))
        group_var = ctx.enter_context(nc.psum_tensor(f"{name}_gv", [MP, MT, NB], F32))
        stats_done, channel_done = sem("stats_done"), sem("channel_done")
        mean_ready, spread_step, var_ready = sem("mean_ready"), sem("spread_step"), sem("var_ready")
        std_ready, rstd_ready, normed = sem("std_ready"), sem("rstd_ready"), sem("normed")
        block = ctx.enter_context(nc.Block())

        @block.vector
        def _(dve):
            for k in range(MT):
                for b in range(NB):
                    for half in range(PX // NX):
                        dve.bn_stats(stats[:, k, b, half, :], src[:, k, b, half * NX:(half + 1) * NX]).then_inc(stats_done, 1)
            for k in range(MT):
                for b in range(NB):
                    dve.wait_ge(stats_done, PX // NX * (k * NB + b + 1))
                    dve.bn_aggr(channel[:, k, b, :], stats[:, k, b, :, :]).then_inc(channel_done, 1)
            dve.wait_ge(mean_ready, 1)
            dve.tensor_copy(t.gn_mean[:, :, :], group_mean[:, :, :]).then_inc(spread_step, 1)
            dve.wait_ge(spread_step, 1)
            dve.tensor_tensor(spread[:, :, :], channel[:, :, :, 0], t.gn_mean[:, :, :], ALU.subtract).then_inc(spread_step, 1)
            dve.wait_ge(spread_step, 2)
            dve.tensor_tensor(spread[:, :, :], spread[:, :, :], spread[:, :, :], ALU.mult).then_inc(spread_step, 1)
            dve.wait_ge(spread_step, 3)
            dve.tensor_tensor(spread[:, :, :], spread[:, :, :], channel[:, :, :, 1], ALU.add).then_inc(spread_step, 1)
            dve.wait_ge(std_ready, 1)
            dve.reciprocal(t.gn_rstd[:, :, :], std[:, :, :]).then_inc(rstd_ready, 1)
            dve.wait_ge(rstd_ready, 1)
            for b in range(NB):
                for k in range(MT):
                    dve.tensor_scalar(dst[:, k, b, :], src[:, k, b, :], t.gn_mean[:, k, b:b + 1], t.gn_rstd[:, k, b:b + 1],
                                      ALU.subtract, ALU.mult).then_inc(normed, 1)

        @block.tensor
        def _(pe):
            pe.wait_ge(channel_done, MT * NB)
            pe.matmul(group_mean[:, :, :], t.group_avg[:, :], channel[:, :, :, 0], start=True, stop=True).then_inc(mean_ready, 1)
            pe.wait_ge(spread_step, 4)
            pe.matmul(group_var[:, :, :], t.group_avg[:, :], spread[:, :, :], start=True, stop=True).then_inc(var_ready, 1)

        @block.scalar
        def _(act):
            act.wait_ge(var_ready, 1)
            act.activation(std[:, :, :], group_var[:, :, :], ACT.Sqrt, bias=t.gn_eps[0:MP, :]).then_inc(std_ready, 1)


def project_and_convolve(nc, t, name, xn, w_in, b_in, conv_w, conv_b, finish, dst):
    VEC, TEN = (0, 1), 2
    TAPS = [(i, j) for i in range(3) for j in range(3)]
    with ExitStack() as ctx:
        sem = lambda what: ctx.enter_context(nc.semaphore(f"{name}_{what}"))
        pad = [ctx.enter_context(nc.sbuf_tensor(f"{name}_pad{c}", [P, HP, WP], F32)) for c in range(CT)]
        diag = ctx.enter_context(nc.sbuf_tensor(f"{name}_diag", [P, len(TAPS), P], F32))
        proj = [ctx.enter_context(nc.psum_tensor(f"{name}_proj{c}", [P, HH, WW], F32)) for c in range(CT)]
        conv_ps = ctx.enter_context(nc.psum_tensor(f"{name}_conv", [P, HH, WW], F32))
        borders, diags = sem("borders"), sem("diags")
        projected = [sem(f"projected{c}") for c in range(CT)]
        padded = [sem(f"padded{c}") for c in range(CT)]
        taps_done = [sem(f"taps_done{c}") for c in VEC]
        conv_ready, finished = sem("conv_ready"), sem("finished")
        block = ctx.enter_context(nc.Block())
        HALVES = [(0, HH // 2), (HH // 2, HH)]

        @block.gpsimd
        def _(pool):
            for c in range(CT):
                pool.memset(pad[c][:, :, :], 0.0).then_inc(borders, 1)
            for k in range(len(TAPS)):
                pool.tensor_scalar(diag[:, k, :], t.ident[:, :], conv_w[:, TEN, k:k + 1], None, ALU.mult).then_inc(diags, 1)

        @block.tensor
        def _(pe):
            for s in (*padded, finished):
                pe.sem_inc(s, 1)
            with pe.Fori(0, NB) as b:
                for c in (TEN, *VEC):
                    pe.wait_ge(padded[c], b + 1)
                    for h0, h1 in HALVES:
                        for k in range(MT):
                            last = pe.matmul(proj[c][:, h0:h1, :], w_in[:, k, c * P:(c + 1) * P],
                                             xn[:, k, b, h0 * WW:h1 * WW], start=(k == 0), stop=(k == MT - 1))
                    last.then_inc(projected[c], 1)
                pe.wait_ge(diags, len(TAPS))
                pe.wait_ge(padded[TEN], b + 2)
                pe.wait_ge(finished, b + 1)
                for h0, h1 in HALVES:
                    for k, (i, j) in enumerate(TAPS):
                        last = pe.matmul(conv_ps[:, h0:h1, :], diag[:, k, :], pad[TEN][:, h0 + i:h1 + i, j:j + WW],
                                         start=(k == 0), stop=(k == len(TAPS) - 1))
                last.then_inc(conv_ready, 1)

        @block.vector
        def _(dve):
            with dve.Fori(0, NB) as b:
                for c in VEC:
                    dve.wait_ge(padded[c], b + 2)
                    for k, (i, j) in enumerate(TAPS):
                        window, out = pad[c][:, i:i + HH, j:j + WW], dst[:, b, c, :, :]
                        if k:
                            dve.wait_ge(taps_done[c], b * len(TAPS) + k)
                            dve.scalar_tensor_tensor(out, window, conv_w[:, c, k:k + 1], out, ALU.mult, ALU.add
                                                     ).then_inc(taps_done[c], 1)
                        elif conv_b is None:
                            dve.tensor_scalar(out, window, conv_w[:, c, k:k + 1], None, ALU.mult).then_inc(taps_done[c], 1)
                        else:
                            dve.tensor_scalar(out, window, conv_w[:, c, k:k + 1], conv_b[:, c:c + 1], ALU.mult, ALU.add
                                              ).then_inc(taps_done[c], 1)

        @block.scalar
        def _(act):
            def pad_image(c, b, reuse):
                act.wait_ge(projected[c], b + 1)
                if reuse:
                    if c == TEN:
                        act.wait_ge(conv_ready, b)
                    else:
                        act.wait_ge(taps_done[c], b * len(TAPS))
                bias = 0.0 if b_in is None else b_in[:, c:c + 1]
                act.activation(pad[c][:, 1:1 + HH, 1:1 + WW], proj[c][:, :, :], ACT.Identity, bias=bias).then_inc(padded[c], 1)

            def finish_image(c, b):
                out = dst[:, b, c, :, :]
                if c == TEN:
                    act.wait_ge(conv_ready, b + 1)
                    bias = 0.0 if conv_b is None else conv_b[:, c:c + 1]
                    act.activation(out, conv_ps[:, :, :], finish, bias=bias).then_inc(finished, 1)
                elif finish != ACT.Identity:
                    act.wait_ge(taps_done[c], (b + 1) * len(TAPS))
                    act.activation(out, out, finish)

            act.wait_ge(borders, CT)
            for c in (TEN, *VEC):
                pad_image(c, 0, False)
            with act.Fori(0, NB - 1) as b:
                finish_image(0, b)
                finish_image(TEN, b)
                pad_image(TEN, b + 1, True)
                pad_image(0, b + 1, True)
                finish_image(1, b)
                pad_image(1, b + 1, True)
            for c in (0, TEN, 1):
                finish_image(c, NB - 1)


def selective_scans(nc, t, u, y):
    with ExitStack() as ctx:
        sem = lambda what: ctx.enter_context(nc.semaphore(f"ssm_{what}"))
        sb = lambda what, shape, dt=F32: ctx.enter_context(nc.sbuf_tensor(f"ssm_{what}", shape, dt))
        a_neg = sb("a_neg", [P, CT, NS])
        a_half = sb("a_half", [P, CT, NS])
        a_slow = sb("a_slow", [P, 2, CT])
        d_skip4 = sb("d_skip4", [P, CT])
        half_ident = sb("half_ident", [P, P])
        seg_mask = sb("seg_mask", [P, SEG, SW])
        carry = sb("carry", [P, NS, CT, SEG])
        xd = sb("xd", [XD, SEG * TC])
        dt = sb("dt", [P, CT, SEG, SW])
        cum = sb("cum", [P, CT, SEG, SW])
        dtu = sb("dtu", [P, CT, SEG, TC])
        gate = sb("gate", [P, CT, SEG, TC])
        decay = sb("decay", [P, CT, SEG, SW])
        drive = sb("drive", [P, CT, SEG, SW])
        h = sb("h", [P, CT, SEG, SW])
        hc = sb("hc", [P, CT, SEG, TC])
        min_cum = sb("min_cum", [P, CT])
        slowest = sb("slowest", [P, 2, CT])
        score = sb("score", [P, 2])
        top = sb("top", [1, 2])
        spare = sb("spare", [1, 2])
        flags = sb("flags", [1, 2], I32)
        ps_y = ctx.enter_context(nc.psum_tensor("ssm_ps_y", [P, CT, SEG, TC], F32))
        ps_bc = ctx.enter_context(nc.psum_tensor("ssm_ps_bc", [P, 2, 2, SEG, TC], F32))
        ps_x = ctx.enter_context(nc.psum_tensor("ssm_ps_x", [P, SEG * TC], F32))

        y_init, setup, a_exp, a_steps = sem("y_init"), sem("setup"), sem("a_exp"), sem("a_steps")
        xdbl_ready, xd_copied, pre_ready = sem("xdbl_ready"), sem("xd_copied"), sem("pre_ready")
        abs_done, exp_done, ln_done = sem("abs_done"), sem("exp_done"), sem("ln_done")
        dt_steps, dt_ready, cum_ready, dtu_ready = sem("dt_steps"), sem("dt_ready"), sem("cum_ready"), sem("dtu_ready")
        score_steps, score_ready, score_rows = sem("score_steps"), sem("score_ready"), sem("score_rows")
        top_ready, flags_ready, added = sem("top_ready"), sem("flags_ready"), sem("added")
        pair = lambda what: [[sem(f"{what}{g}{c}") for c in range(CT)] for g in range(2)]
        bc_ready = [sem("bc_ready0"), sem("bc_ready1")]
        tanh_done, gate_ready, gated = pair("tanh_done"), pair("gate_ready"), pair("gated")
        driven, scanned, hc_ready, summed = pair("driven"), pair("scanned"), pair("hc_ready"), pair("summed")
        saved = pair("saved")
        block = ctx.enter_context(nc.Block())

        def along(v, c, direction, k=slice(None)):
            v = v[:, :, :, :, :].rearrange("p b k h w -> p k b h w")
            i = c if direction in FORWARD else HH - 1 - c
            return v[:, k, :, i, :] if direction in BY_ROW else v[:, k, :, :, i]

        def at_ends(v, k, forward, backward):
            whole = v[:, :, :, :]
            (parts, tile, seg) = whole.ap[0], whole.ap[1], whole.ap[2]
            tiles = [[tile[0], len(k)]] if len(k) > 1 else []
            return bass.AP(tensor=whole.tensor, offset=whole.offset + k[0] * tile[0] + forward,
                           ap=[parts, *tiles, [seg[0] * SEG // 2 + backward - forward, 2], [seg[0], SEG // 2]])

        START, END = (0, SW - 1), (TC, 1)
        halves = lambda v: v.rearrange("p (f s) -> p f s", f=2)

        segs = lambda direction: slice(direction * NB, (direction + 1) * NB)
        before = lambda c, n: c * (NS - 1) + n - 1

        def settle(eng, semaphore, count):
            eng.wait_ge(semaphore, 1)
            eng.wait_ge(semaphore, count)

        def chunks(eng, work, rest, close):
            live = [eng.alloc_register(f"live_any_{eng.engine}"), eng.alloc_register(f"live_rest_{eng.engine}")]
            for reg in live:
                eng.reg_mov(reg, 1)
            with eng.Fori(0, HH // CHUNK_GROUP) as group:
                with eng.If_ne(live[0], 0):
                    with eng.Fori(0, CHUNK_GROUP) as i:
                        c = group * CHUNK_GROUP + i
                        with eng.If_ne(live[0], 0):
                            work(c)
                            with eng.If_ne(live[1], 0):
                                rest(c)
                            close(c)
                            settle(eng, flags_ready, c + 1)
                            for j, reg in enumerate(live):
                                eng.reg_load(reg, flags[0:1, j:j + 1])
                        eng.nop()
                eng.nop()

        def states(eng, unit):
            with eng.Fori(1, NS - 1, 2) as n:
                unit(n, 1)
                unit(n + 1, 0)
            unit(NS - 1, 1)

        @block.gpsimd
        def _(pool):
            for k in range(CT):
                pool.wait_ge(a_steps, 1)
                pool.tensor_scalar(y[:, :, k, :, :], u[:, :, k, :, :], d_skip4[:, k:k + 1], 1.0, ALU.mult, ALU.mult
                                   ).then_inc(y_init, 1)

            def unit(c, n, g, count):
                for k in range(CT):
                    if g:
                        pool.wait_ge(scanned[1][k], 2 * count + 1)
                    pool.tensor_tensor(at_ends(drive, [k], *START), halves(carry[:, n, k, :]), halves(seg_mask[:, :, 1]), ALU.mult
                                       ).then_inc(gated[g][k], 1)
                    pool.wait_ge(gate_ready[g][k], count + 1)
                    pool.tensor_tensor(gate[:, k, :, :], gate[:, k, :, :], dtu[:, k, :, :], ALU.mult).then_inc(gated[g][k], 1)

            def work(c):
                pool.wait_ge(dt_ready, c + 1)
                for r in range(NDIR):
                    pool.tensor_tensor(dtu[:, :, segs(r), :], dt[:, :, segs(r), 1:1 + TC], along(u, c, r), ALU.mult
                                       ).then_inc(dtu_ready, 1)
                settle(pool, dtu_ready, NDIR * c + NDIR)
                unit(c, 0, 0, c)

            def rest(c):
                for k in range(CT):
                    pool.wait_ge(scanned[0][k], 2 * c + 2)
                pool.tensor_tensor(spare[:, 1:2], seg_mask[0:1, 0, 0:1], seg_mask[0:1, 0, 0:1], ALU.mult)
                states(pool, lambda n, parity: unit(c, n, 1, before(c, n)))

            chunks(pool, work, rest, lambda c: None)

        @block.scalar
        def _(act):
            act.activation(a_neg[:, :, :], t.a_log, ACT.Exp).then_inc(a_exp, 1)

            def unit(n, g, count):
                for k in range(CT):
                    if g:
                        act.wait_ge(scanned[1][k], 2 * count + 1)
                    act.activation(gate[:, k, :, :], cum[:, k, :, 1:1 + TC], ACT.Tanh, bias=t.half_log_guard[:, :],
                                   scale=a_half[:, k, bass.ds(n, 1)]).then_inc(tanh_done[g][k], 1)
                    act.activation(decay[:, k, :, 1:1 + TC], dt[:, k, :, 1:1 + TC], ACT.Exp, scale=a_neg[:, k, bass.ds(n, 1)])
                    act.wait_ge(tanh_done[g][k], count + 1)
                    act.activation(gate[:, k, :, :], gate[:, k, :, :], ACT.Identity, bias=1.0).then_inc(gate_ready[g][k], 1)

            def work(c):
                act.wait_ge(xdbl_ready, c + 1)
                act.activation(xd[:, :], ps_x[0:XD, :], ACT.Copy).then_inc(xd_copied, 1)
                for k in range(CT):
                    act.wait_ge(pre_ready, CT * c + k + 1)
                    act.activation(gate[:, k, :, :], ps_y[:, k, :, :], ACT.Abs, bias=t.b_dt[:, k:k + 1]).then_inc(abs_done, 1)
                act.wait_ge(abs_done, CT * c + CT)
                act.activation(gate[:, :, :, :], gate[:, :, :, :], ACT.Exp, scale=-1.0).then_inc(exp_done, 1)
                act.wait_ge(exp_done, c + 1)
                act.activation(dtu[:, :, :, :], gate[:, :, :, :], ACT.Ln, bias=1.0).then_inc(ln_done, 1)
                act.wait_ge(a_steps, 3)
                act.wait_ge(cum_ready, 2 * CT * c + 2 * CT)
                unit(0, 0, c)

            def rest(c):
                for k in range(CT):
                    act.wait_ge(scanned[0][k], 2 * c + 2)
                states(act, lambda n, parity: unit(n, 1, before(c, n)))

            chunks(act, work, rest, lambda c: None)

        @block.tensor
        def _(pe):
            for s in (*scanned[1], *summed[1], added):
                pe.sem_inc(s, 1)

            def spread(n, parity, g):
                for j in range(2):
                    row = RK + j * NS + n
                    last = pe.matmul(ps_bc[:, parity, j, :, :], t.ident[0:XD, row:row + 1].broadcast_to([XD, P]), xd[:, :],
                                     start=True, stop=True)
                last.then_inc(bc_ready[g], 1)

            def add_up(g, count):
                for k in range(CT):
                    pe.wait_ge(hc_ready[g][k], count + 1)
                    pe.matmul(ps_y[:, k, :, :], half_ident[:, :], hc[:, k, :, :], start=(g == 0), stop=(g == 0),
                              skip_group_check=True).then_inc(summed[g][k], 1)

            def work(c):
                pe.wait_ge(added, NDIR * c + 1)
                for r in range(NDIR):
                    for k in range(CT):
                        last = pe.matmul(ps_x[0:XD, r * NB * TC:(r + 1) * NB * TC], t.w_x[:, k, :], along(u, c, r, k),
                                         start=(k == 0), stop=(k == CT - 1))
                last.then_inc(xdbl_ready, 1)
                pe.wait_ge(xd_copied, c + 1)
                for k in range(CT):
                    pe.matmul(ps_y[:, k, :, :], t.w_dt[:, k * P:(k + 1) * P], xd[0:RK, :], start=True, stop=True
                              ).then_inc(pre_ready, 1)
                spread(0, 0, 0)
                pe.wait_ge(setup, SETUP)
                pe.wait_ge(score_ready, c + 1)
                for j in range(2):
                    last = pe.matmul(ps_x[0:1, j * P:(j + 1) * P], score[:, j:j + 1], t.ident, start=True, stop=True)
                last.then_inc(score_rows, 1)
                add_up(0, c)

            def rest(c):
                spread(1, 1, 1)
                for n in range(1, NS):
                    if n + 1 < NS:
                        spread(n + 1, (n + 1) % 2, 1)
                    add_up(1, before(c, n))

            chunks(pe, work, rest, lambda c: None)

        @block.vector
        def _(dve):
            dve.tensor_scalar(d_skip4[:, :], t.d_skip, float(NDIR), None, ALU.mult).then_inc(a_steps, 1)
            dve.wait_ge(a_exp, 1)
            dve.tensor_scalar(a_half[:, :, :], a_neg[:, :, :], -0.5, None, ALU.mult).then_inc(a_steps, 1)
            dve.wait_ge(a_steps, 2)
            dve.tensor_scalar(a_neg[:, :, :], a_neg[:, :, :], -1.0, None, ALU.mult).then_inc(a_steps, 1)
            dve.wait_ge(a_steps, 3)
            dve.tensor_reduce(a_slow[:, 0, :], a_neg[:, :, :], AX.X, ALU.max).then_inc(a_steps, 1)
            dve.tensor_reduce(a_slow[:, 1, :], a_neg[:, :, 1:], AX.X, ALU.max).then_inc(a_steps, 1)
            dve.memset(seg_mask[:, :, :], 1.0).then_inc(setup, 1)
            dve.memset(carry[:, :, :, :], 0.0).then_inc(setup, 1)
            for v in (decay, drive, dt, cum):
                dve.memset(v[:, :, :, :], 0.0).then_inc(setup, 1)
            dve.tensor_scalar(half_ident[:, :], t.ident, 0.5, None, ALU.mult).then_inc(setup, 1)
            dve.wait_ge(setup, SETUP)
            for end in START:
                dve.memset(seg_mask[:, :, end], 0.0).then_inc(a_steps, 1)
            dve.wait_ge(a_steps, 7)

            def scan(out, factor, term, done):
                for part in (slice(0, SEG // 2), slice(SEG // 2, SEG)):
                    lines = [v[:, part, :].rearrange("p s w -> p (s w)") for v in (out, factor, term)]
                    if part.start:
                        lines = [v[:, ::-1] for v in lines]
                    dve.tensor_tensor_scan(*lines, 0.0, ALU.mult, ALU.add).then_inc(done, 1)

            def unit(n, parity, g, count):
                for k in range(CT):
                    if k == 0:
                        dve.wait_ge(bc_ready[g], count + 1)
                    dve.wait_ge(gated[g][k], 2 * count + 2)
                    dve.tensor_tensor(drive[:, k, :, 1:1 + TC], gate[:, k, :, :], ps_bc[:, parity, 0, :, :], ALU.mult
                                      ).then_inc(driven[g][k], 1)
                    dve.wait_ge(driven[g][k], count + 1)
                    scan(h[:, k, :, :], decay[:, k, :, :], drive[:, k, :, :], scanned[g][k])
                    dve.wait_ge(scanned[g][k], 2 * count + 2 + g)
                    if g:
                        dve.wait_ge(summed[1][k], count + 1)
                    dve.tensor_tensor(hc[:, k, :, :], h[:, k, :, 1:1 + TC], ps_bc[:, parity, 1, :, :], ALU.mult
                                      ).then_inc(hc_ready[g][k], 1)
                    dve.tensor_copy(halves(carry[:, n, k, :]), at_ends(h, [k], *END)).then_inc(saved[g][k], 1)

            def work(c):
                for k in range(CT):
                    dve.wait_ge(abs_done, CT * c + k + 1)
                    dve.tensor_scalar(dt[:, k, :, 1:1 + TC], ps_y[:, k, :, :], t.b_dt[:, k:k + 1], 0.0, ALU.add, ALU.max
                                      ).then_inc(dt_steps, 1)
                dve.tensor_copy(at_ends(dt, range(CT), *START), at_ends(cum, range(CT), *END)).then_inc(dt_steps, 1)
                dve.wait_ge(exp_done, c + 1)
                dve.tensor_scalar(drive[:, :, :, 1:1 + TC], gate[:, :, :, :], 1.0, -1.0, ALU.add, ALU.add).then_inc(dt_steps, 1)
                dve.wait_ge(dt_steps, 7 * c + 5)
                dve.tensor_tensor(drive[:, :, :, 1:1 + TC], gate[:, :, :, :], drive[:, :, :, 1:1 + TC], ALU.subtract).then_inc(dt_steps, 1)
                dve.wait_ge(ln_done, c + 1)
                dve.wait_ge(dt_steps, 7 * c + 6)
                dve.tensor_tensor(drive[:, :, :, 1:1 + TC], drive[:, :, :, 1:1 + TC], dtu[:, :, :, :], ALU.add).then_inc(dt_steps, 1)
                dve.wait_ge(dt_steps, 7 * c + 7)
                dve.tensor_tensor(dt[:, :, :, 1:1 + TC], dt[:, :, :, 1:1 + TC], drive[:, :, :, 1:1 + TC], ALU.add).then_inc(dt_ready, 1)
                dve.wait_ge(dt_ready, c + 1)
                for k in range(CT):
                    scan(cum[:, k, :, :], seg_mask[:, :, :], dt[:, k, :, :], cum_ready)
                dve.wait_ge(cum_ready, 2 * CT * c + 2 * CT)
                dve.tensor_reduce(min_cum[:, :], at_ends(cum, range(CT), *END), AX.XY, ALU.min).then_inc(score_steps, 1)
                dve.wait_ge(score_steps, 3 * c + 1)
                for j in range(2):
                    dve.tensor_tensor(slowest[:, j, :], a_slow[:, j, :], min_cum[:, :], ALU.mult).then_inc(score_steps, 1)
                dve.wait_ge(score_steps, 3 * c + 3)
                dve.tensor_reduce(score[:, :], slowest[:, :, :], AX.X, ALU.max).then_inc(score_ready, 1)
                unit(0, 0, 0, c)
                dve.wait_ge(score_rows, c + 1)
                dve.tensor_reduce(top[:, :], ps_x[0:1, 0:2 * P].rearrange("p (j n) -> p j n", j=2), AX.X, ALU.max
                                  ).then_inc(top_ready, 1)
                dve.wait_ge(top_ready, c + 1)
                dve.tensor_scalar(flags[:, :], top[:, :], DEAD, None, ALU.is_gt).then_inc(flags_ready, 1)

            def rest(c):
                for k in range(CT):
                    settle(dve, summed[0][k], c + 1)
                states(dve, lambda n, parity: unit(n, parity, 1, before(c, n)))
                for k in range(CT):
                    dve.wait_ge(summed[1][k], before(c, NS) + 1)
                    dve.wait_ge(saved[1][k], before(c, NS))
                dve.memset(spare[:, 0:1], 0.0)

            def close(c):
                dve.wait_ge(y_init, CT)
                for k in range(CT):
                    settle(dve, summed[0][k], c + 1)
                    settle(dve, saved[0][k], c + 1)
                for place, r in enumerate(sorted(range(NDIR), key=lambda r: r not in BY_ROW)):
                    if place == NDIR // 2:
                        dve.wait_ge(added, NDIR * c + place + 1)
                        dve.memset(spare[:, 0:1], 0.0)
                    dve.tensor_tensor(along(y, c, r), ps_y[:, :, segs(r), :], along(y, c, r), ALU.add).then_inc(added, 1)

            chunks(dve, work, rest, close)


def channel_norm(nc, name, ctx, y, gamma):
    sem = lambda what: ctx.enter_context(nc.semaphore(f"{name}_{what}"))
    s = Names()
    s.mean_ready, s.centred, s.squared, s.var_ready = sem("mean_ready"), sem("centred"), sem("squared"), sem("var_ready")
    s.log_done, s.rstd_ready, s.scaled = sem("log_done"), sem("rstd_ready"), sem("scaled")
    square = ctx.enter_context(nc.sbuf_tensor(f"{name}_square", [P, CT, NX], F32))
    rstd = ctx.enter_context(nc.sbuf_tensor(f"{name}_rstd", [P, NX], F32))
    mean_ps = ctx.enter_context(nc.psum_tensor(f"{name}_mean", [P, NX], F32))
    var_ps = ctx.enter_context(nc.psum_tensor(f"{name}_var", [P, NX], F32))
    rows = HH // 2

    def part(b, half, k=slice(None)):
        return y[:, b, k, half * rows:(half + 1) * rows, :]

    def flat(b, half):
        return part(b, half).rearrange("p k h w -> p k (h w)")

    def mean(pe, avg, b, half, done):
        pe.wait_ge(s.centred, done)
        for k in range(CT):
            last = pe.matmul(mean_ps[:, :], avg, part(b, half, k), start=(k == 0), stop=(k == CT - 1))
        last.then_inc(s.mean_ready, 1)

    def centre(dve, b, half, done):
        dve.wait_ge(s.mean_ready, done + 1)
        dve.tensor_tensor(flat(b, half), flat(b, half), mean_ps[:, None, :].broadcast_to([P, CT, NX]), ALU.subtract
                          ).then_inc(s.centred, 1)

    def squares(act, b, half, done):
        act.wait_ge(s.centred, done + 1)
        act.wait_ge(s.var_ready, done)
        act.activation(square[:, :, :], flat(b, half), ACT.Square).then_inc(s.squared, 1)

    def variance(pe, avg, done):
        pe.wait_ge(s.squared, done + 1)
        pe.wait_ge(s.log_done, done)
        for k in range(CT):
            last = pe.matmul(var_ps[:, :], avg, square[:, k, :], start=(k == 0), stop=(k == CT - 1))
        last.then_inc(s.var_ready, 1)

    def reciprocal_std(act, eps, done):
        act.wait_ge(s.var_ready, done + 1)
        act.wait_ge(s.scaled, CT * done)
        act.activation(rstd[:, :], var_ps[:, :], ACT.Ln, bias=eps).then_inc(s.log_done, 1)
        act.wait_ge(s.log_done, done + 1)
        act.activation(rstd[:, :], rstd[:, :], ACT.Exp, scale=-0.5).then_inc(s.rstd_ready, 1)

    def scale(dve, b, half, done):
        dve.wait_ge(s.rstd_ready, done + 1)
        for k in range(CT):
            here = part(b, half, k).rearrange("p h w -> p (h w)")
            dve.scalar_tensor_tensor(here, here, gamma[:, k:k + 1], rstd[:, :], ALU.mult, ALU.mult).then_inc(s.scaled, 1)

    s.part, s.flat = part, flat
    s.mean, s.centre, s.squares, s.variance, s.reciprocal_std, s.scale = (
        mean, centre, squares, variance, reciprocal_std, scale)
    return s


def norm_gate_project(nc, t, sems, d, y, xn, x):
    with ExitStack() as ctx:
        sem = lambda what: ctx.enter_context(nc.semaphore(f"gate_{what}"))
        norm = channel_norm(nc, "gate", ctx, y, t.gamma0)
        gate = ctx.enter_context(nc.sbuf_tensor("gate_silu", [P, CT, NX], F32))
        z_ps = ctx.enter_context(nc.psum_tensor("gate_z", [P, CT, NX], F32))
        out_ps = ctx.enter_context(nc.psum_tensor("gate_out", [MP, MT, NX], F32))
        normed, z_ready, silu_done = sem("normed"), sem("z_ready"), sem("silu_done")
        gated, projected, residual_done = sem("gated"), sem("projected"), sem("residual_done")
        block = ctx.enter_context(nc.Block())
        avg, eps = t.avg_inner[:, :], t.gn_eps[:, :]
        cols = lambda half: slice(half * NX, (half + 1) * NX)

        @block.sync
        def _(sp):
            for b in range(NB):
                sp.dma_start(x[:, :, b, :], d["x"].rearrange("(k p) (b n) -> p k b n", p=MP, b=NB)[:, :, b, :]
                             ).then_inc(sems.x_again[b], 16)

        @block.tensor
        def _(pe):
            def z(b, half, done):
                pe.wait_ge(normed, MT * b + MT)
                pe.wait_ge(silu_done, done)
                for c in range(CT):
                    for k in range(MT):
                        last = pe.matmul(z_ps[:, c, :], t.w_in0[:, k, DI + c * P:DI + (c + 1) * P], xn[:, k, b, cols(half)],
                                         start=(k == 0), stop=(k == MT - 1))
                last.then_inc(z_ready, 1)

            def project(b, half, done):
                pe.wait_ge(gated, CT * done + CT)
                pe.wait_ge(residual_done, done)
                for m in range(MT):
                    for k in range(CT):
                        last = pe.matmul(out_ps[:, m, :], t.w_out0[:, k, m * MP:(m + 1) * MP], norm.part(b, half, k),
                                         start=(k == 0), stop=(k == CT - 1))
                last.then_inc(projected, 1)

            def front(b, half, done):
                norm.mean(pe, avg, b, half, done)
                z(b, half, done)
                norm.variance(pe, avg, done)

            front(0, 0, 0)
            with pe.Fori(0, NB - 1) as b:
                front(b, 1, 2 * b + 1)
                project(b, 0, 2 * b)
                front(b + 1, 0, 2 * b + 2)
                project(b, 1, 2 * b + 1)
            front(NB - 1, 1, 2 * NB - 1)
            project(NB - 1, 0, 2 * NB - 2)
            project(NB - 1, 1, 2 * NB - 1)

        @block.scalar
        def _(act):
            def step(b, half, done):
                norm.squares(act, b, half, done)
                act.wait_ge(z_ready, done + 1)
                act.wait_ge(gated, CT * done)
                act.activation(gate[:, :, :], z_ps[:, :, :], ACT.Silu).then_inc(silu_done, 1)
                norm.reciprocal_std(act, eps, done)

            step(0, 0, 0)
            with act.Fori(0, NB - 1) as b:
                step(b, 1, 2 * b + 1)
                step(b + 1, 0, 2 * b + 2)
            step(NB - 1, 1, 2 * NB - 1)

        @block.vector
        def _(dve):
            for b in range(NB):
                dve.wait_ge(sems.x_again[b], 16)
                for k in range(MT):
                    dve.tensor_scalar(xn[:, k, b, :], x[:, k, b, :], t.gn_mean[:, k, b:b + 1], t.gn_rstd[:, k, b:b + 1],
                                      ALU.subtract, ALU.mult).then_inc(normed, 1)

            def residual(b, half, done):
                dve.wait_ge(projected, done + 1)
                dve.tensor_tensor(x[:, :, b, cols(half)], out_ps[:, :, :], x[:, :, b, cols(half)], ALU.add
                                  ).then_inc(residual_done, 1)

            def step(b, half, done):
                norm.centre(dve, b, half, done)
                norm.scale(dve, b, half, done)
                dve.wait_ge(silu_done, done + 1)
                for k in range(CT):
                    here = norm.part(b, half, k).rearrange("p h w -> p (h w)")
                    dve.wait_ge(norm.scaled, CT * done + k + 1)
                    dve.scalar_tensor_tensor(here, here, t.beta0[:, k:k + 1], gate[:, k, :], ALU.add, ALU.mult).then_inc(gated, 1)

            step(0, 0, 0)
            with dve.Fori(0, NB - 1) as b:
                step(b, 1, 2 * b + 1)
                residual(b, 0, 2 * b)
                step(b + 1, 0, 2 * b + 2)
                residual(b, 1, 2 * b + 1)
            step(NB - 1, 1, 2 * NB - 1)
            residual(NB - 1, 0, 2 * NB - 2)
            residual(NB - 1, 1, 2 * NB - 1)


def moving_averages(nc, y):
    GROUP = 2
    with ExitStack() as ctx:
        sem = lambda what: ctx.enter_context(nc.semaphore(f"ema_{what}"))
        f = [ctx.enter_context(nc.sbuf_tensor(f"ema_{axis}", [P, GROUP * CT, HH, WW], F32)) for axis in ("rows", "columns")]
        steps = [sem("steps_rows"), sem("steps_columns")]
        mixed = sem("mixed")
        block = ctx.enter_context(nc.Block())
        PER = 2 * HH

        @block.vector
        def _(dve):
            def at(v, axis, i):
                return v[:, :, i, :] if axis == 0 else v[:, :, :, i]

            dve.sem_inc(mixed, 1)
            with dve.Fori(0, NB // GROUP) as g:
                x = y[:, bass.ds(g * GROUP, GROUP), :, :, :].rearrange("p b k h w -> p (b k) h w")
                for axis in range(2):
                    dve.wait_ge(mixed, 2 * g + 1)
                    dve.tensor_scalar(at(f[axis], axis, 0), at(x, axis, 0), 1.0, None, ALU.mult).then_inc(steps[axis], 1)
                for i in range(1, HH):
                    for axis in range(2):
                        dve.wait_ge(steps[axis], PER * g + i)
                        dve.scalar_tensor_tensor(at(f[axis], axis, i), at(f[axis], axis, i - 1), DECAY, at(x, axis, i),
                                                 ALU.mult, ALU.add).then_inc(steps[axis], 1)
                for axis in range(2):
                    dve.wait_ge(steps[axis], PER * g + HH)
                    last = at(f[axis], axis, HH - 1)
                    dve.tensor_scalar(last, last, 1 / (1 - DECAY ** 2), None, ALU.mult).then_inc(steps[axis], 1)
                for i in range(HH - 2, -1, -1):
                    for axis in range(2):
                        dve.wait_ge(steps[axis], PER * g + 2 * HH - 1 - i)
                        dve.scalar_tensor_tensor(at(f[axis], axis, i), at(f[axis], axis, i + 1), DECAY, at(f[axis], axis, i),
                                                 ALU.mult, ALU.add).then_inc(steps[axis], 1)
                whole = x.rearrange("p c h w -> p (c h w)")
                scale_x = (1 + GAIN / 2) / (GAIN / 4 * (1 - DECAY ** 2))
                dve.wait_ge(steps[0], PER * g + PER)
                dve.scalar_tensor_tensor(whole, whole, scale_x, f[0][:, :, :, :].rearrange("p c h w -> p (c h w)"),
                                         ALU.mult, ALU.add).then_inc(mixed, 1)
                dve.wait_ge(steps[1], PER * g + PER)
                dve.wait_ge(mixed, 2 * g + 2)
                dve.tensor_tensor(whole, whole, f[1][:, :, :, :].rearrange("p c h w -> p (c h w)"), ALU.add).then_inc(mixed, 1)


def norm_project_out(nc, t, sems, out, y, x):
    with ExitStack() as ctx:
        sem = lambda what: ctx.enter_context(nc.semaphore(f"final_{what}"))
        norm = channel_norm(nc, "final", ctx, y, t.gamma1)
        shift = ctx.enter_context(nc.sbuf_tensor("final_shift", [MP, MT], F32))
        shift_ps = ctx.enter_context(nc.psum_tensor("final_shift_ps", [MP, MT], F32))
        out_ps = ctx.enter_context(nc.psum_tensor("final_out", [MP, MT, NX], F32))
        shift_product, shift_ready, projected, added = sem("shift_product"), sem("shift_ready"), sem("projected"), sem("added")
        block = ctx.enter_context(nc.Block())
        avg, eps = t.avg_inner[:, :], t.gn_eps[:, :]
        cols = lambda half: slice(half * NX, (half + 1) * NX)

        @block.tensor
        def _(pe):
            for m in range(MT):
                for k in range(CT):
                    last = pe.matmul(shift_ps[:, m:m + 1], t.w_out1[:, k, m * MP:(m + 1) * MP], t.beta1[:, k:k + 1],
                                     start=(k == 0), stop=(k == CT - 1))
            last.then_inc(shift_product, 1)

            def project(b, half, done):
                pe.wait_ge(norm.scaled, CT * done + CT)
                pe.wait_ge(added, MT * done)
                for m in range(MT):
                    for k in range(CT):
                        last = pe.matmul(out_ps[:, m, :], t.w_out1[:, k, m * MP:(m + 1) * MP], norm.part(b, half, k),
                                         start=(k == 0), stop=(k == CT - 1))
                last.then_inc(projected, 1)

            def front(b, half, done):
                norm.mean(pe, avg, b, half, done)
                norm.variance(pe, avg, done)

            front(0, 0, 0)
            with pe.Fori(0, NB - 1) as b:
                front(b, 1, 2 * b + 1)
                project(b, 0, 2 * b)
                front(b + 1, 0, 2 * b + 2)
                project(b, 1, 2 * b + 1)
            front(NB - 1, 1, 2 * NB - 1)
            project(NB - 1, 0, 2 * NB - 2)
            project(NB - 1, 1, 2 * NB - 1)

        @block.scalar
        def _(act):
            def step(b, half, done):
                norm.squares(act, b, half, done)
                norm.reciprocal_std(act, eps, done)

            step(0, 0, 0)
            with act.Fori(0, NB - 1) as b:
                step(b, 1, 2 * b + 1)
                step(b + 1, 0, 2 * b + 2)
            step(NB - 1, 1, 2 * NB - 1)

        @block.vector
        def _(dve):
            dve.wait_ge(shift_product, 1)
            dve.tensor_tensor(shift[:, :], shift_ps[:, :], t.b_out1, ALU.add).then_inc(shift_ready, 1)
            dve.wait_ge(shift_ready, 1)

            def residual(b, half, done):
                dve.wait_ge(projected, done + 1)
                for m in range(MT):
                    here = x[:, m, b, cols(half)]
                    dve.scalar_tensor_tensor(here, out_ps[:, m, :], shift[:, m:m + 1], here, ALU.add, ALU.add).then_inc(added, 1)

            def step(b, half, done):
                norm.centre(dve, b, half, done)
                norm.scale(dve, b, half, done)

            step(0, 0, 0)
            with dve.Fori(0, NB - 1) as b:
                step(b, 1, 2 * b + 1)
                residual(b, 0, 2 * b)
                step(b + 1, 0, 2 * b + 2)
                residual(b, 1, 2 * b + 1)
            step(NB - 1, 1, 2 * NB - 1)
            residual(NB - 1, 0, 2 * NB - 2)
            residual(NB - 1, 1, 2 * NB - 1)

        @block.sync
        def _(sp):
            for b in range(NB):
                sp.wait_ge(added, 2 * MT * (b + 1))
                sp.dma_start(out.rearrange("(k p) (b n) -> p k b n", p=MP, b=NB)[:, :, b, :], x[:, :, b, :]
                             ).then_inc(sems.out_done, 16)
            sp.wait_ge(sems.out_done, 16 * NB)


def build(nc, d, out):
    with ExitStack() as ctx:
        sb = lambda name, shape, dt=F32: ctx.enter_context(nc.sbuf_tensor(name, shape, dt))
        sem = lambda name: ctx.enter_context(nc.semaphore(name))
        sems = Names()
        sems.x_in = [sem(f"x_in{b}") for b in range(NB)]
        sems.x_again = [sem(f"x_again{b}") for b in range(NB)]
        sems.params, sems.fills, sems.out_done = sem("params"), sem("fills"), sem("out_done")
        t = Names()
        t.inner_params = sb("inner_params", [P, sum(INNER.values())])
        t.model_params = sb("model_params", [MP, sum(MODEL.values())])
        t.w_dt = sb("w_dt", [RK, DI])
        t.avg_inner = sb("avg_inner", [P, P])
        t.gn_eps, t.half_log_guard = sb("gn_eps", [P, 1]), sb("half_log_guard", [P, 1])
        t.gn_mean, t.gn_rstd = sb("gn_mean", [MP, MT, NB]), sb("gn_rstd", [MP, MT, NB])
        inner, model = unpack(t.inner_params, INNER), unpack(t.model_params, MODEL)
        t.conv_w0, t.conv_w1, t.conv_b0 = inner["conv_w0"], inner["conv_w1"], inner["conv_b0"]
        t.w_x, t.a_log, t.b_dt, t.d_skip = inner["w_x"], inner["a_log"], inner["b_dt"], inner["d_skip"]
        t.w_out0, t.w_out1, t.b_in1, t.ident = inner["w_out0"], inner["w_out1"], inner["b_in1"], inner["ident"]
        t.gamma0, t.beta0, t.gamma1, t.beta1 = inner["gamma0"], inner["beta0"], inner["gamma1"], inner["beta1"]
        t.w_in0, t.w_in1, t.b_out1, t.group_avg = model["w_in0"], model["w_in1"], model["b_out1"], model["group_avg"]
        u = sb("u", [P, NB, CT, HH, WW])
        y = sb("y", [P, NB, CT, HH, WW])
        stages(nc, t, sems, d, out, u, y)


def stages(nc, t, sems, d, out, u, y):
    with nc.sbuf_tensor("xn0", [MP, MT, NB, PX], F32) as xn:
        t.x = xn
        load(nc, t, sems, d)
        group_norm(nc, t, "gn0", xn, xn)
        project_and_convolve(nc, t, "conv0", xn, t.w_in0, None, t.conv_w0, t.conv_b0, ACT.Silu, u)
    selective_scans(nc, t, u, y)
    x = u[0:MP, :, :, :, :].rearrange("p b k h w -> p (b k h w)")[:, 0:MT * NPOS].rearrange(
        "p (k b n) -> p k b n", k=MT, b=NB)
    with nc.sbuf_tensor("xn1", [MP, MT, NB, PX], F32) as xn:
        norm_gate_project(nc, t, sems, d, y, xn, x)
        group_norm(nc, t, "gn1", x, xn)
        project_and_convolve(nc, t, "conv1", xn, t.w_in1, t.b_in1, t.conv_w1, None, ACT.Identity, y)
    moving_averages(nc, y)
    norm_project_out(nc, t, sems, out, y, x)


_SOURCES = {"conv_w0": "L0_conv_conv_w", "conv_w1": "L1_conv_conv_w", "w_x": "L0_conv_W_x", "a_log": "L0_conv_A_log",
            "w_out0": "L0_conv_W_out", "w_out1": "L1_conv_W_out", "conv_b0": "L0_conv_conv_b", "b_dt": "L0_conv_b_dt",
            "d_skip": "L0_conv_D_param", "gamma0": "L0_conv_gamma", "beta0": "L0_conv_beta", "b_in1": "L1_conv_b_in",
            "gamma1": "L1_conv_ln_g", "beta1": "L1_conv_ln_b", "w_in0": "L0_conv_W_in", "w_in1": "L1_conv_W_in",
            "b_out1": "L1_conv_b_out"}


def kernel(**inputs):
    import numpy as np
    import concourse.bacc as bacc
    from concourse.bass_utils import run_bass_kernel_spmd as run

    nc = bacc.Bacc("TRN2", target_bir_lowering=False, num_devices=1)
    fixed = {"ident": np.eye(P, dtype=np.float32),
             "group_avg": np.kron(np.eye(MP // 6, dtype=np.float32), np.full((6, 6), 1 / 6, np.float32))}

    def pack(columns, rows):
        parts = [fixed[n] if n in fixed else
                 inputs[_SOURCES[n]].reshape(inputs[_SOURCES[n]].shape[0] // rows, rows, -1).transpose(1, 0, 2).reshape(rows, w)
                 for n, w in columns.items()]
        return np.ascontiguousarray(np.concatenate(parts, axis=1))

    arrays = {"x": np.ascontiguousarray(inputs["x"].reshape(NPOS, DM).T), "w_dt": np.ascontiguousarray(inputs["L0_conv_W_dt"]),
              "inner_params": pack(INNER, P), "model_params": pack(MODEL, MP)}
    maps, d = {}, {}
    for name, a in arrays.items():
        maps[f"in_{name}"] = a
        d[name] = nc.dram_tensor(f"in_{name}", a.shape, F32, kind="ExternalInput").ap()
    out = nc.dram_tensor("out", (DM, NPOS), F32, kind="ExternalOutput").ap()
    build(nc, d, out)
    r = run(nc, [maps], core_ids=[0])
    return np.ascontiguousarray(r.results[0]["out"].T).reshape(NB, HH, WW, DM)
```

```python
from contextlib import ExitStack

import concourse.bass as bass
from concourse import mybir

F32 = mybir.dt.float32
I32 = mybir.dt.int32
ALU = mybir.AluOpType
ACT = mybir.ActivationFunctionType
AX = mybir.AxisListType

NB, HH, WW, DM = 4, 32, 32, 192
DI, NS, RK = 384, 16, 12
PX = HH * WW
NPOS = NB * PX
P = 128
CT = DI // P
MP, MT = 96, DM // 96
NX = 512
HP, WP = HH + 2, WW + 2
XD = RK + 2 * NS
GN_EPS, LN_EPS = 1e-5, 1e-5
DECAY, GAIN = 0.6, 0.4
TC = 32
NDIR = 4
SEG = NDIR * NB
SW = TC + 2
FORWARD, BY_ROW = (0, 1), (0, 2)
SETUP = 7
GUARD = 1e-12
HALF_LOG_GUARD = 13.815510557964274
CHUNK_GROUP = 4
DEAD = -104.0


class Names:
    pass


INNER = {"conv_w0": CT * 9, "conv_w1": CT * 9, "w_x": CT * XD, "a_log": CT * NS, "w_out0": CT * DM, "w_out1": CT * DM,
         "conv_b0": CT, "b_dt": CT, "d_skip": CT, "gamma0": CT, "beta0": CT, "b_in1": CT, "gamma1": CT, "beta1": CT,
         "ident": P}
MODEL = {"w_in0": MT * 2 * DI, "w_in1": MT * DI, "b_out1": MT, "group_avg": MP}


def unpack(packed, columns):
    parts, at = {}, 0
    for name, n in columns.items():
        tiles = 1 if name in ("ident", "group_avg") else CT if columns is INNER else MT
        part = packed[:, at:at + n]
        parts[name] = part if tiles == 1 or n == tiles else part.rearrange("p (t n) -> p t n", t=tiles)
        at += n
    return parts


def load(nc, t, sems, d):
    with nc.Block() as block:

        @block.sync
        def _(sp):
            for b in range(NB):
                sp.dma_start(t.x[:, :, b, :], d["x"].rearrange("(k p) (b n) -> p k b n", p=MP, b=NB)[:, :, b, :]
                             ).then_inc(sems.x_in[b], 16)
            for b in range(NB):
                sp.wait_ge(sems.x_in[b], 16)

        @block.scalar
        def _(act):
            act.dma_start(t.model_params[:, :], d["model_params"]).then_inc(sems.params, 16)
            act.dma_start(t.inner_params[:, :], d["inner_params"]).then_inc(sems.params, 16)
            act.dma_start(t.w_dt[:, :], d["w_dt"]).then_inc(sems.params, 16)
            act.wait_ge(sems.params, 16 * 3)

        @block.gpsimd
        def _(pool):
            pool.memset(t.avg_inner[:, :], 1.0 / DI).then_inc(sems.fills, 1)
            pool.memset(t.gn_eps[:, :], GN_EPS).then_inc(sems.fills, 1)
            pool.memset(t.half_log_guard[:, :], HALF_LOG_GUARD).then_inc(sems.fills, 1)
            pool.wait_ge(sems.params, 16 * 3)
            pool.tensor_scalar(t.conv_w1, t.conv_w1, GAIN / 4 * (1 - DECAY ** 2), 1.0, ALU.mult, ALU.mult).then_inc(sems.fills, 1)
            pool.wait_ge(sems.fills, 4)


def group_norm(nc, t, name, src, dst):
    with ExitStack() as ctx:
        sem = lambda what: ctx.enter_context(nc.semaphore(f"{name}_{what}"))
        sb = lambda what, shape: ctx.enter_context(nc.sbuf_tensor(f"{name}_{what}", shape, F32))
        stats = sb("stats", [MP, MT, NB, PX // NX, 6])
        channel = sb("channel", [MP, MT, NB, 2])
        spread = sb("spread", [MP, MT, NB])
        std = sb("std", [MP, MT, NB])
        group_mean = ctx.enter_context(nc.psum_tensor(f"{name}_gm", [MP, MT, NB], F32))
        group_var = ctx.enter_context(nc.psum_tensor(f"{name}_gv", [MP, MT, NB], F32))
        stats_done, channel_done = sem("stats_done"), sem("channel_done")
        mean_ready, spread_step, var_ready = sem("mean_ready"), sem("spread_step"), sem("var_ready")
        std_ready, rstd_ready, normed = sem("std_ready"), sem("rstd_ready"), sem("normed")
        block = ctx.enter_context(nc.Block())

        @block.vector
        def _(dve):
            for k in range(MT):
                for b in range(NB):
                    for half in range(PX // NX):
                        dve.bn_stats(stats[:, k, b, half, :], src[:, k, b, half * NX:(half + 1) * NX]).then_inc(stats_done, 1)
            for k in range(MT):
                for b in range(NB):
                    dve.wait_ge(stats_done, PX // NX * (k * NB + b + 1))
                    dve.bn_aggr(channel[:, k, b, :], stats[:, k, b, :, :]).then_inc(channel_done, 1)
            dve.wait_ge(mean_ready, 1)
            dve.tensor_copy(t.gn_mean[:, :, :], group_mean[:, :, :]).then_inc(spread_step, 1)
            dve.wait_ge(spread_step, 1)
            dve.tensor_tensor(spread[:, :, :], channel[:, :, :, 0], t.gn_mean[:, :, :], ALU.subtract).then_inc(spread_step, 1)
            dve.wait_ge(spread_step, 2)
            dve.tensor_tensor(spread[:, :, :], spread[:, :, :], spread[:, :, :], ALU.mult).then_inc(spread_step, 1)
            dve.wait_ge(spread_step, 3)
            dve.tensor_tensor(spread[:, :, :], spread[:, :, :], channel[:, :, :, 1], ALU.add).then_inc(spread_step, 1)
            dve.wait_ge(std_ready, 1)
            dve.reciprocal(t.gn_rstd[:, :, :], std[:, :, :]).then_inc(rstd_ready, 1)
            dve.wait_ge(rstd_ready, 1)
            for b in range(NB):
                for k in range(MT):
                    dve.tensor_scalar(dst[:, k, b, :], src[:, k, b, :], t.gn_mean[:, k, b:b + 1], t.gn_rstd[:, k, b:b + 1],
                                      ALU.subtract, ALU.mult).then_inc(normed, 1)

        @block.tensor
        def _(pe):
            pe.wait_ge(channel_done, MT * NB)
            pe.matmul(group_mean[:, :, :], t.group_avg[:, :], channel[:, :, :, 0], start=True, stop=True).then_inc(mean_ready, 1)
            pe.wait_ge(spread_step, 4)
            pe.matmul(group_var[:, :, :], t.group_avg[:, :], spread[:, :, :], start=True, stop=True).then_inc(var_ready, 1)

        @block.scalar
        def _(act):
            act.wait_ge(var_ready, 1)
            act.activation(std[:, :, :], group_var[:, :, :], ACT.Sqrt, bias=t.gn_eps[0:MP, :]).then_inc(std_ready, 1)


def project_and_convolve(nc, t, name, xn, w_in, b_in, conv_w, conv_b, finish, dst):
    VEC, TEN = (0, 1), 2
    TAPS = [(i, j) for i in range(3) for j in range(3)]
    with ExitStack() as ctx:
        sem = lambda what: ctx.enter_context(nc.semaphore(f"{name}_{what}"))
        pad = [ctx.enter_context(nc.sbuf_tensor(f"{name}_pad{c}", [P, HP, WP], F32)) for c in range(CT)]
        diag = ctx.enter_context(nc.sbuf_tensor(f"{name}_diag", [P, len(TAPS), P], F32))
        proj = [ctx.enter_context(nc.psum_tensor(f"{name}_proj{c}", [P, HH, WW], F32)) for c in range(CT)]
        conv_ps = ctx.enter_context(nc.psum_tensor(f"{name}_conv", [P, HH, WW], F32))
        borders, diags = sem("borders"), sem("diags")
        projected = [sem(f"projected{c}") for c in range(CT)]
        padded = [sem(f"padded{c}") for c in range(CT)]
        taps_done = [sem(f"taps_done{c}") for c in VEC]
        conv_ready, finished = sem("conv_ready"), sem("finished")
        block = ctx.enter_context(nc.Block())
        HALVES = [(0, HH // 2), (HH // 2, HH)]

        @block.gpsimd
        def _(pool):
            for c in range(CT):
                pool.memset(pad[c][:, :, :], 0.0).then_inc(borders, 1)
            for k in range(len(TAPS)):
                pool.tensor_scalar(diag[:, k, :], t.ident[:, :], conv_w[:, TEN, k:k + 1], None, ALU.mult).then_inc(diags, 1)

        @block.tensor
        def _(pe):
            for s in (*padded, finished):
                pe.sem_inc(s, 1)
            with pe.Fori(0, NB) as b:
                for c in (TEN, *VEC):
                    pe.wait_ge(padded[c], b + 1)
                    for h0, h1 in HALVES:
                        for k in range(MT):
                            last = pe.matmul(proj[c][:, h0:h1, :], w_in[:, k, c * P:(c + 1) * P],
                                             xn[:, k, b, h0 * WW:h1 * WW], start=(k == 0), stop=(k == MT - 1))
                    last.then_inc(projected[c], 1)
                pe.wait_ge(diags, len(TAPS))
                pe.wait_ge(padded[TEN], b + 2)
                pe.wait_ge(finished, b + 1)
                for h0, h1 in HALVES:
                    for k, (i, j) in enumerate(TAPS):
                        last = pe.matmul(conv_ps[:, h0:h1, :], diag[:, k, :], pad[TEN][:, h0 + i:h1 + i, j:j + WW],
                                         start=(k == 0), stop=(k == len(TAPS) - 1))
                last.then_inc(conv_ready, 1)

        @block.vector
        def _(dve):
            with dve.Fori(0, NB) as b:
                for c in VEC:
                    dve.wait_ge(padded[c], b + 2)
                    for k, (i, j) in enumerate(TAPS):
                        window, out = pad[c][:, i:i + HH, j:j + WW], dst[:, b, c, :, :]
                        if k:
                            dve.wait_ge(taps_done[c], b * len(TAPS) + k)
                            dve.scalar_tensor_tensor(out, window, conv_w[:, c, k:k + 1], out, ALU.mult, ALU.add
                                                     ).then_inc(taps_done[c], 1)
                        elif conv_b is None:
                            dve.tensor_scalar(out, window, conv_w[:, c, k:k + 1], None, ALU.mult).then_inc(taps_done[c], 1)
                        else:
                            dve.tensor_scalar(out, window, conv_w[:, c, k:k + 1], conv_b[:, c:c + 1], ALU.mult, ALU.add
                                              ).then_inc(taps_done[c], 1)

        @block.scalar
        def _(act):
            def pad_image(c, b, reuse):
                act.wait_ge(projected[c], b + 1)
                if reuse:
                    if c == TEN:
                        act.wait_ge(conv_ready, b)
                    else:
                        act.wait_ge(taps_done[c], b * len(TAPS))
                bias = 0.0 if b_in is None else b_in[:, c:c + 1]
                act.activation(pad[c][:, 1:1 + HH, 1:1 + WW], proj[c][:, :, :], ACT.Identity, bias=bias).then_inc(padded[c], 1)

            def finish_image(c, b):
                out = dst[:, b, c, :, :]
                if c == TEN:
                    act.wait_ge(conv_ready, b + 1)
                    bias = 0.0 if conv_b is None else conv_b[:, c:c + 1]
                    act.activation(out, conv_ps[:, :, :], finish, bias=bias).then_inc(finished, 1)
                elif finish != ACT.Identity:
                    act.wait_ge(taps_done[c], (b + 1) * len(TAPS))
                    act.activation(out, out, finish)

            act.wait_ge(borders, CT)
            for c in (TEN, *VEC):
                pad_image(c, 0, False)
            with act.Fori(0, NB - 1) as b:
                finish_image(0, b)
                finish_image(TEN, b)
                pad_image(TEN, b + 1, True)
                pad_image(0, b + 1, True)
                finish_image(1, b)
                pad_image(1, b + 1, True)
            for c in (0, TEN, 1):
                finish_image(c, NB - 1)


def settle(eng, semaphore, count):
    eng.wait_ge(semaphore, 1)
    eng.wait_ge(semaphore, count)


def after(eng, semaphore, count):
    if not isinstance(count, int) or count > 0:
        eng.wait_ge(semaphore, count)


def selective_scans(nc, t, u, y):
    with ExitStack() as ctx:
        sem = lambda what: ctx.enter_context(nc.semaphore(f"ssm_{what}"))
        sb = lambda what, shape, dt=F32: ctx.enter_context(nc.sbuf_tensor(f"ssm_{what}", shape, dt))
        a_neg = sb("a_neg", [P, CT, NS])
        a_half = sb("a_half", [P, CT, NS])
        a_slow = sb("a_slow", [P, 2, CT])
        d_skip4 = sb("d_skip4", [P, CT])
        half_ident = sb("half_ident", [P, P])
        seg_mask = sb("seg_mask", [P, SEG, SW])
        carry = sb("carry", [P, NS, CT, SEG])
        xd = sb("xd", [XD, SEG * TC])
        dt = sb("dt", [P, CT, SEG, SW])
        cum = sb("cum", [P, CT, SEG, SW])
        dtu = sb("dtu", [P, CT, SEG, TC])
        gate = sb("gate", [P, CT, SEG, TC])
        decay = sb("decay", [P, CT, SEG, SW])
        drive = sb("drive", [P, CT, SEG, SW])
        h = sb("h", [P, CT, SEG, SW])
        hc = sb("hc", [P, CT, SEG, TC])
        min_cum = sb("min_cum", [P, CT])
        slowest = sb("slowest", [P, 2, CT])
        score = sb("score", [P, 2])
        top = sb("top", [1, 2])
        spare = sb("spare", [1, 2])
        flags = sb("flags", [1, 2], I32)
        ps_y = ctx.enter_context(nc.psum_tensor("ssm_ps_y", [P, CT, SEG, TC], F32))
        ps_bc = ctx.enter_context(nc.psum_tensor("ssm_ps_bc", [P, 2, 2, SEG, TC], F32))
        ps_x = ctx.enter_context(nc.psum_tensor("ssm_ps_x", [P, SEG * TC], F32))

        y_init, setup, a_exp, a_steps = sem("y_init"), sem("setup"), sem("a_exp"), sem("a_steps")
        xdbl_ready, xd_copied, pre_ready = sem("xdbl_ready"), sem("xd_copied"), sem("pre_ready")
        abs_done, exp_done, ln_done = sem("abs_done"), sem("exp_done"), sem("ln_done")
        dt_steps, dt_ready, cum_ready, dtu_ready = sem("dt_steps"), sem("dt_ready"), sem("cum_ready"), sem("dtu_ready")
        score_steps, score_ready, score_rows = sem("score_steps"), sem("score_ready"), sem("score_rows")
        top_ready, flags_ready, added = sem("top_ready"), sem("flags_ready"), sem("added")
        pair = lambda what: [[sem(f"{what}{g}{c}") for c in range(CT)] for g in range(2)]
        bc_ready = [sem("bc_ready0"), sem("bc_ready1")]
        tanh_done, gate_ready, gated = pair("tanh_done"), pair("gate_ready"), pair("gated")
        driven, scanned, hc_ready, summed = pair("driven"), pair("scanned"), pair("hc_ready"), pair("summed")
        saved = pair("saved")
        block = ctx.enter_context(nc.Block())

        def along(v, c, direction, k=slice(None)):
            v = v[:, :, :, :, :].rearrange("p b k h w -> p k b h w")
            i = c if direction in FORWARD else HH - 1 - c
            return v[:, k, :, i, :] if direction in BY_ROW else v[:, k, :, :, i]

        def at_ends(v, k, forward, backward):
            whole = v[:, :, :, :]
            (parts, tile, seg) = whole.ap[0], whole.ap[1], whole.ap[2]
            tiles = [[tile[0], len(k)]] if len(k) > 1 else []
            return bass.AP(tensor=whole.tensor, offset=whole.offset + k[0] * tile[0] + forward,
                           ap=[parts, *tiles, [seg[0] * SEG // 2 + backward - forward, 2], [seg[0], SEG // 2]])

        START, END = (0, SW - 1), (TC, 1)
        halves = lambda v: v.rearrange("p (f s) -> p f s", f=2)

        segs = lambda direction: slice(direction * NB, (direction + 1) * NB)
        before = lambda c, n: c * (NS - 1) + n - 1

        def chunks(eng, work, rest, close):
            live = [eng.alloc_register(f"live_any_{eng.engine}"), eng.alloc_register(f"live_rest_{eng.engine}")]
            for reg in live:
                eng.reg_mov(reg, 1)
            with eng.Fori(0, HH // CHUNK_GROUP) as group:
                with eng.If_ne(live[0], 0):
                    with eng.Fori(0, CHUNK_GROUP) as i:
                        c = group * CHUNK_GROUP + i
                        with eng.If_ne(live[0], 0):
                            work(c)
                            with eng.If_ne(live[1], 0):
                                rest(c)
                            close(c)
                            settle(eng, flags_ready, c + 1)
                            for j, reg in enumerate(live):
                                eng.reg_load(reg, flags[0:1, j:j + 1])
                        eng.nop()
                eng.nop()

        def states(eng, unit):
            with eng.Fori(1, NS - 1, 2) as n:
                unit(n, 1)
                unit(n + 1, 0)
            unit(NS - 1, 1)

        @block.gpsimd
        def _(pool):
            for k in range(CT):
                pool.wait_ge(a_steps, 1)
                pool.tensor_scalar(y[:, :, k, :, :], u[:, :, k, :, :], d_skip4[:, k:k + 1], 1.0, ALU.mult, ALU.mult
                                   ).then_inc(y_init, 1)

            def unit(c, n, g, count):
                for k in range(CT):
                    if g:
                        pool.wait_ge(scanned[1][k], 2 * count + 1)
                    pool.tensor_tensor(at_ends(drive, [k], *START), halves(carry[:, n, k, :]), halves(seg_mask[:, :, 1]), ALU.mult
                                       ).then_inc(gated[g][k], 1)
                    pool.wait_ge(gate_ready[g][k], count + 1)
                    pool.tensor_tensor(gate[:, k, :, :], gate[:, k, :, :], dtu[:, k, :, :], ALU.mult).then_inc(gated[g][k], 1)

            def work(c):
                pool.wait_ge(dt_ready, c + 1)
                for r in range(NDIR):
                    pool.tensor_tensor(dtu[:, :, segs(r), :], dt[:, :, segs(r), 1:1 + TC], along(u, c, r), ALU.mult
                                       ).then_inc(dtu_ready, 1)
                settle(pool, dtu_ready, NDIR * c + NDIR)
                unit(c, 0, 0, c)

            def rest(c):
                for k in range(CT):
                    pool.wait_ge(scanned[0][k], 2 * c + 2)
                pool.tensor_tensor(spare[:, 1:2], seg_mask[0:1, 0, 0:1], seg_mask[0:1, 0, 0:1], ALU.mult)
                states(pool, lambda n, parity: unit(c, n, 1, before(c, n)))

            chunks(pool, work, rest, lambda c: None)

        @block.scalar
        def _(act):
            act.activation(a_neg[:, :, :], t.a_log, ACT.Exp).then_inc(a_exp, 1)

            def unit(n, g, count):
                for k in range(CT):
                    if g:
                        act.wait_ge(scanned[1][k], 2 * count + 1)
                    act.activation(gate[:, k, :, :], cum[:, k, :, 1:1 + TC], ACT.Tanh, bias=t.half_log_guard[:, :],
                                   scale=a_half[:, k, bass.ds(n, 1)]).then_inc(tanh_done[g][k], 1)
                    act.activation(decay[:, k, :, 1:1 + TC], dt[:, k, :, 1:1 + TC], ACT.Exp, scale=a_neg[:, k, bass.ds(n, 1)])
                    act.wait_ge(tanh_done[g][k], count + 1)
                    act.activation(gate[:, k, :, :], gate[:, k, :, :], ACT.Identity, bias=1.0).then_inc(gate_ready[g][k], 1)

            def work(c):
                act.wait_ge(xdbl_ready, c + 1)
                act.activation(xd[:, :], ps_x[0:XD, :], ACT.Copy).then_inc(xd_copied, 1)
                for k in range(CT):
                    act.wait_ge(pre_ready, CT * c + k + 1)
                    act.activation(gate[:, k, :, :], ps_y[:, k, :, :], ACT.Abs, bias=t.b_dt[:, k:k + 1]).then_inc(abs_done, 1)
                act.wait_ge(abs_done, CT * c + CT)
                act.activation(gate[:, :, :, :], gate[:, :, :, :], ACT.Exp, scale=-1.0).then_inc(exp_done, 1)
                act.wait_ge(exp_done, c + 1)
                act.activation(dtu[:, :, :, :], gate[:, :, :, :], ACT.Ln, bias=1.0).then_inc(ln_done, 1)
                act.wait_ge(a_steps, 3)
                act.wait_ge(cum_ready, 2 * CT * c + 2 * CT)
                unit(0, 0, c)

            def rest(c):
                for k in range(CT):
                    act.wait_ge(scanned[0][k], 2 * c + 2)
                states(act, lambda n, parity: unit(n, 1, before(c, n)))

            chunks(act, work, rest, lambda c: None)

        @block.tensor
        def _(pe):
            for s in (*scanned[1], *summed[1], added):
                pe.sem_inc(s, 1)

            def spread(n, parity, g):
                for j in range(2):
                    row = RK + j * NS + n
                    last = pe.matmul(ps_bc[:, parity, j, :, :], t.ident[0:XD, row:row + 1].broadcast_to([XD, P]), xd[:, :],
                                     start=True, stop=True)
                last.then_inc(bc_ready[g], 1)

            def add_up(g, count):
                for k in range(CT):
                    pe.wait_ge(hc_ready[g][k], count + 1)
                    pe.matmul(ps_y[:, k, :, :], half_ident[:, :], hc[:, k, :, :], start=(g == 0), stop=(g == 0),
                              skip_group_check=True).then_inc(summed[g][k], 1)

            def work(c):
                pe.wait_ge(added, NDIR * c + 1)
                for r in range(NDIR):
                    for k in range(CT):
                        last = pe.matmul(ps_x[0:XD, r * NB * TC:(r + 1) * NB * TC], t.w_x[:, k, :], along(u, c, r, k),
                                         start=(k == 0), stop=(k == CT - 1))
                last.then_inc(xdbl_ready, 1)
                pe.wait_ge(xd_copied, c + 1)
                for k in range(CT):
                    pe.matmul(ps_y[:, k, :, :], t.w_dt[:, k * P:(k + 1) * P], xd[0:RK, :], start=True, stop=True
                              ).then_inc(pre_ready, 1)
                spread(0, 0, 0)
                pe.wait_ge(setup, SETUP)
                pe.wait_ge(score_ready, c + 1)
                for j in range(2):
                    last = pe.matmul(ps_x[0:1, j * P:(j + 1) * P], score[:, j:j + 1], t.ident, start=True, stop=True)
                last.then_inc(score_rows, 1)
                add_up(0, c)

            def rest(c):
                spread(1, 1, 1)
                for n in range(1, NS):
                    if n + 1 < NS:
                        spread(n + 1, (n + 1) % 2, 1)
                    add_up(1, before(c, n))

            chunks(pe, work, rest, lambda c: None)

        @block.vector
        def _(dve):
            dve.tensor_scalar(d_skip4[:, :], t.d_skip, float(NDIR), None, ALU.mult).then_inc(a_steps, 1)
            dve.wait_ge(a_exp, 1)
            dve.tensor_scalar(a_half[:, :, :], a_neg[:, :, :], -0.5, None, ALU.mult).then_inc(a_steps, 1)
            dve.wait_ge(a_steps, 2)
            dve.tensor_scalar(a_neg[:, :, :], a_neg[:, :, :], -1.0, None, ALU.mult).then_inc(a_steps, 1)
            dve.wait_ge(a_steps, 3)
            dve.tensor_reduce(a_slow[:, 0, :], a_neg[:, :, :], AX.X, ALU.max).then_inc(a_steps, 1)
            dve.tensor_reduce(a_slow[:, 1, :], a_neg[:, :, 1:], AX.X, ALU.max).then_inc(a_steps, 1)
            dve.memset(seg_mask[:, :, :], 1.0).then_inc(setup, 1)
            dve.memset(carry[:, :, :, :], 0.0).then_inc(setup, 1)
            for v in (decay, drive, dt, cum):
                dve.memset(v[:, :, :, :], 0.0).then_inc(setup, 1)
            dve.tensor_scalar(half_ident[:, :], t.ident, 0.5, None, ALU.mult).then_inc(setup, 1)
            dve.wait_ge(setup, SETUP)
            for end in START:
                dve.memset(seg_mask[:, :, end], 0.0).then_inc(a_steps, 1)
            dve.wait_ge(a_steps, 7)

            def scan(out, factor, term, done):
                for part in (slice(0, SEG // 2), slice(SEG // 2, SEG)):
                    lines = [v[:, part, :].rearrange("p s w -> p (s w)") for v in (out, factor, term)]
                    if part.start:
                        lines = [v[:, ::-1] for v in lines]
                    dve.tensor_tensor_scan(*lines, 0.0, ALU.mult, ALU.add).then_inc(done, 1)

            def unit(n, parity, g, count):
                for k in range(CT):
                    if k == 0:
                        dve.wait_ge(bc_ready[g], count + 1)
                    dve.wait_ge(gated[g][k], 2 * count + 2)
                    dve.tensor_tensor(drive[:, k, :, 1:1 + TC], gate[:, k, :, :], ps_bc[:, parity, 0, :, :], ALU.mult
                                      ).then_inc(driven[g][k], 1)
                    dve.wait_ge(driven[g][k], count + 1)
                    scan(h[:, k, :, :], decay[:, k, :, :], drive[:, k, :, :], scanned[g][k])
                    dve.wait_ge(scanned[g][k], 2 * count + 2 + g)
                    if g:
                        dve.wait_ge(summed[1][k], count + 1)
                    dve.tensor_tensor(hc[:, k, :, :], h[:, k, :, 1:1 + TC], ps_bc[:, parity, 1, :, :], ALU.mult
                                      ).then_inc(hc_ready[g][k], 1)
                    dve.tensor_copy(halves(carry[:, n, k, :]), at_ends(h, [k], *END)).then_inc(saved[g][k], 1)

            def work(c):
                for k in range(CT):
                    dve.wait_ge(abs_done, CT * c + k + 1)
                    dve.tensor_scalar(dt[:, k, :, 1:1 + TC], ps_y[:, k, :, :], t.b_dt[:, k:k + 1], 0.0, ALU.add, ALU.max
                                      ).then_inc(dt_steps, 1)
                dve.tensor_copy(at_ends(dt, range(CT), *START), at_ends(cum, range(CT), *END)).then_inc(dt_steps, 1)
                dve.wait_ge(exp_done, c + 1)
                dve.tensor_scalar(drive[:, :, :, 1:1 + TC], gate[:, :, :, :], 1.0, -1.0, ALU.add, ALU.add).then_inc(dt_steps, 1)
                dve.wait_ge(dt_steps, 7 * c + 5)
                dve.tensor_tensor(drive[:, :, :, 1:1 + TC], gate[:, :, :, :], drive[:, :, :, 1:1 + TC], ALU.subtract).then_inc(dt_steps, 1)
                dve.wait_ge(ln_done, c + 1)
                dve.wait_ge(dt_steps, 7 * c + 6)
                dve.tensor_tensor(drive[:, :, :, 1:1 + TC], drive[:, :, :, 1:1 + TC], dtu[:, :, :, :], ALU.add).then_inc(dt_steps, 1)
                dve.wait_ge(dt_steps, 7 * c + 7)
                dve.tensor_tensor(dt[:, :, :, 1:1 + TC], dt[:, :, :, 1:1 + TC], drive[:, :, :, 1:1 + TC], ALU.add).then_inc(dt_ready, 1)
                dve.wait_ge(dt_ready, c + 1)
                for k in range(CT):
                    scan(cum[:, k, :, :], seg_mask[:, :, :], dt[:, k, :, :], cum_ready)
                dve.wait_ge(cum_ready, 2 * CT * c + 2 * CT)
                dve.tensor_reduce(min_cum[:, :], at_ends(cum, range(CT), *END), AX.XY, ALU.min).then_inc(score_steps, 1)
                dve.wait_ge(score_steps, 3 * c + 1)
                for j in range(2):
                    dve.tensor_tensor(slowest[:, j, :], a_slow[:, j, :], min_cum[:, :], ALU.mult).then_inc(score_steps, 1)
                dve.wait_ge(score_steps, 3 * c + 3)
                dve.tensor_reduce(score[:, :], slowest[:, :, :], AX.X, ALU.max).then_inc(score_ready, 1)
                unit(0, 0, 0, c)
                dve.wait_ge(score_rows, c + 1)
                dve.tensor_reduce(top[:, :], ps_x[0:1, 0:2 * P].rearrange("p (j n) -> p j n", j=2), AX.X, ALU.max
                                  ).then_inc(top_ready, 1)
                dve.wait_ge(top_ready, c + 1)
                dve.tensor_scalar(flags[:, :], top[:, :], DEAD, None, ALU.is_gt).then_inc(flags_ready, 1)

            def rest(c):
                for k in range(CT):
                    settle(dve, summed[0][k], c + 1)
                states(dve, lambda n, parity: unit(n, parity, 1, before(c, n)))
                for k in range(CT):
                    dve.wait_ge(summed[1][k], before(c, NS) + 1)
                    dve.wait_ge(saved[1][k], before(c, NS))
                dve.memset(spare[:, 0:1], 0.0)

            def close(c):
                dve.wait_ge(y_init, CT)
                for k in range(CT):
                    settle(dve, summed[0][k], c + 1)
                    settle(dve, saved[0][k], c + 1)
                for place, r in enumerate(sorted(range(NDIR), key=lambda r: r not in BY_ROW)):
                    if place == NDIR // 2:
                        dve.wait_ge(added, NDIR * c + place + 1)
                        dve.memset(spare[:, 0:1], 0.0)
                    dve.tensor_tensor(along(y, c, r), ps_y[:, :, segs(r), :], along(y, c, r), ALU.add).then_inc(added, 1)

            chunks(dve, work, rest, close)



EXP_AND_LN = 6


def gate_mix_and_project(nc, t, sems, d, out, y, u):
    VEC, TEN = (0, 1), 2
    TAPS = [(i, j) for i in range(3) for j in range(3)]
    ROWS = HH // 2
    ITEMS = 2 * CT
    MIX_X = (1 + GAIN / 2) / (GAIN / 4 * (1 - DECAY ** 2))
    with ExitStack() as ctx:
        sem = lambda what: ctx.enter_context(nc.semaphore(f"t_{what}"))
        sb = lambda what, shape: ctx.enter_context(nc.sbuf_tensor(f"t_{what}", shape, F32))
        psum = lambda what, shape: ctx.enter_context(nc.psum_tensor(f"t_{what}", shape, F32))
        whole_u = u[:, :, :, :, :].rearrange("p b k h w -> p (b k h w)")
        x = whole_u[0:MP, 0:MT * NPOS].rearrange("p (k b n) -> p k b n", k=MT, b=NB)
        turned = whole_u[:, MT * NPOS:MT * NPOS + CT * PX].rearrange("p (k w h) -> p k w h", k=CT, w=WW)
        factor = whole_u[:, MT * NPOS + CT * PX:].rearrange("p (l i) -> p l i", i=WW)
        xz, xn = sb("xz", [MP, MT, PX]), sb("xn", [MP, MT, PX])
        pad = [sb(f"pad{c}", [P, HP, WP]) for c in range(CT)]
        diag = sb("diag", [P, len(TAPS), P])
        square, gate = sb("square", [P, CT, NX]), sb("gate", [P, 2, CT, NX])
        sum_y, sum_square, rstd = sb("sum_y", [P, 2, NX]), sb("sum_square", [P, NX]), sb("rstd", [P, NX])
        ema = [sb("ema_w", [P, CT, HH, WW]), sb("ema_h", [P, CT, WW, HH])]
        stats, channel = sb("stats", [MP, MT, 2, 6]), sb("channel", [MP, MT, 2])
        group_mean, spread, group_rstd = sb("group_mean", [MP, MT]), sb("spread", [MP, MT]), sb("group_rstd", [MP, MT])
        shift, spare = sb("shift", [MP, MT]), sb("spare", [1, 64])
        mean_ps, var_ps = psum("mean_ps", [P, NX]), psum("var_ps", [P, NX])
        out_ps = psum("out_ps", [MP, MT, NX])
        ring = psum("ring", [P, 2, NX])
        conv_ps = psum("conv_ps", [P, 2, ROWS, WW])
        group_ps = conv_ps[0:MP, 0, 0, 0:MT]

        borders, diags, factors, shift_product, shift_ready = (
            sem("borders"), sem("diags"), sem("factors"), sem("shift_product"), sem("shift_ready"))
        sum_y_done, mean_ready, centred, squared = sem("sum_y_done"), sem("mean_ready"), sem("centred"), sem("squared")
        sum_square_done, var_ready, log_done, rstd_ready = (
            sem("sum_square_done"), sem("var_ready"), sem("log_done"), sem("rstd_ready"))
        scaled, gated, projected, out_read = sem("scaled"), sem("gated"), sem("projected"), sem("out_read")
        xz_ready, ring_ready, ring_read = sem("xz_ready"), sem("ring_ready"), sem("ring_read")
        stats_done, channel_done, group_steps = sem("stats_done"), sem("channel_done"), sem("group_steps")
        group_mean_ready, group_var_ready, group_log, group_rstd_ready = (
            sem("group_mean_ready"), sem("group_var_ready"), sem("group_log"), sem("group_rstd_ready"))
        xn_ready = sem("xn_ready")
        taps_done = [sem(f"taps_done{c}") for c in VEC]
        conv_ready, conv_read, turned_ready = sem("conv_ready"), sem("conv_read"), sem("turned_ready")
        ema_steps = [sem("ema_w_steps"), sem("ema_h_steps")]
        mixed_rows, mixed_columns = sem("mixed_rows"), [sem(f"mixed_columns{k}") for k in range(CT)]
        block = ctx.enter_context(nc.Block())

        avg, eps = t.avg_inner[:, :], t.gn_eps[:, :]
        cols = lambda half: slice(half * NX, (half + 1) * NX)
        rows = lambda half: slice(half * ROWS, (half + 1) * ROWS)
        part = lambda b, half, k=slice(None): y[:, b, k, rows(half), :]
        line = lambda b, half, k: part(b, half, k).rearrange("p h w -> p (h w)")
        lines = lambda b, half: part(b, half).rearrange("p k h w -> p k (h w)")

        inner = lambda image, excepted: not isinstance(image, int) or image not in excepted

        def z_item(j, half, c):
            return (2 * ITEMS * j - ITEMS if inner(j, (0,)) else 0) + half * CT + c

        def pad_item(i, c, half):
            return 2 * ITEMS * i + (2 * ITEMS if inner(i, (NB - 1,)) else ITEMS) + 2 * c + half

        def gate_n(j, half):
            return (4 * j - 4 if inner(j, (0, 1)) else 2 * j) + half

        def final_n(b, half):
            return 4 * b + (6 if inner(b, (NB - 2, NB - 1)) else 4 if b == NB - 2 else 2) + half

        places = iter(range(64))

        def free_place():
            place = next(places)
            return spare[:, place:place + 1]

        carry_waits_pool = lambda: nc.gpsimd.tensor_tensor(free_place(), t.ident[0:1, 0:1], t.ident[0:1, 0:1], ALU.mult)
        carry_waits_act = lambda: nc.scalar.activation(free_place(), t.ident[0:1, 0:1], ACT.Copy)
        carry_waits_dve = lambda: nc.vector.memset(free_place(), 0.0)

        def mix_columns(eng, b, k):
            eng.wait_ge(mixed_rows, b + 1)
            eng.wait_ge(ema_steps[1], (2 * CT + 1) * (b + 1))
            if eng is nc.gpsimd:
                carry_waits_pool()
            eng.tensor_tensor(y[:, b, k, :, :], y[:, b, k, :, :], ema[1][:, k, :, :].rearrange("p w h -> p h w"), ALU.add
                              ).then_inc(mixed_columns[k], 1)

        @block.sync
        def _(sp):
            for b in range(NB):
                sp.dma_start(x[:, :, b, :], d["x"].rearrange("(k p) (b n) -> p k b n", p=MP, b=NB)[:, :, b, :]
                             ).then_inc(sems.x_again[b], 16)
            for b in range(NB):
                sp.wait_ge(out_read, 2 * final_n(b, 1) + 2)
                sp.dma_start(out.rearrange("(k p) (b n) -> p k b n", p=MP, b=NB)[:, :, b, :], x[:, :, b, :]
                             ).then_inc(sems.out_done, 16)
            sp.wait_ge(sems.out_done, 16 * NB)

        @block.gpsimd
        def _(pool):
            def sums_of_tiles(b, half, n):
                after(pool, mean_ready, n - 1)
                carry_waits_pool()
                here = sum_y[:, half, :]
                pool.tensor_tensor(here, line(b, half, 0), line(b, half, 1), ALU.add).then_inc(sum_y_done, 1)
                pool.wait_ge(sum_y_done, 2 * n + 1)
                carry_waits_pool()
                pool.tensor_tensor(here, here, line(b, half, 2), ALU.add).then_inc(sum_y_done, 1)

            def sums_of_squares(n):
                pool.wait_ge(squared, n + 1)
                after(pool, var_ready, n)
                pool.tensor_tensor(sum_square[:, :], square[:, 0, :], square[:, 1, :], ALU.add).then_inc(sum_square_done, 1)
                pool.wait_ge(sum_square_done, 2 * n + 1)
                pool.tensor_tensor(sum_square[:, :], sum_square[:, :], square[:, 2, :], ALU.add).then_inc(sum_square_done, 1)

            def turn(b, j):
                if j is not None:
                    for half in range(2):
                        sums_of_tiles(j, half, gate_n(j, half))
                    for half in range(2):
                        sums_of_squares(gate_n(j, half))
                if b is not None:
                    mix_columns(pool, b, TEN)
                    for c in range(CT):
                        pool.wait_ge(mixed_columns[c], b + 1)
                    for half in range(2):
                        sums_of_tiles(b, half, final_n(b, half))
                    for half in range(2):
                        sums_of_squares(final_n(b, half))

            turn(None, 0)
            for c in range(CT):
                pool.memset(pad[c][:, :, :], 0.0).then_inc(borders, 1)
            for k in range(len(TAPS)):
                pool.tensor_scalar(diag[:, k, :], t.ident, t.conv_w1[:, TEN, k:k + 1], 1.0, ALU.mult, ALU.mult).then_inc(diags, 1)
            turn(None, 1)
            with pool.Fori(1, NB - 1) as i:
                turn(i - 1, i + 1)
            turn(NB - 2, None)
            turn(NB - 1, None)

        @block.scalar
        def _(act):
            def load_exp_ln():
                act.add_instruction(mybir.InstLoadActFuncSet(name=nc.get_next_instruction_name(), act_func_set_id=EXP_AND_LN))

            def squares(b, half, n):
                act.wait_ge(centred, n + 1)
                after(act, sum_square_done, 2 * n)
                act.activation(square[:, :, :], lines(b, half), ACT.Square).then_inc(squared, 1)

            def reciprocal_std(n):
                act.wait_ge(var_ready, n + 1)
                after(act, scaled, CT * n)
                act.activation(rstd[:, :], var_ps[:, :], ACT.Ln, bias=eps).then_inc(log_done, 1)
                act.wait_ge(log_done, n + 1)
                act.activation(rstd[:, :], rstd[:, :], ACT.Exp, scale=-0.5).then_inc(rstd_ready, 1)

            def silu_z(i, half):
                for c in range(CT):
                    j = z_item(0, half, c)
                    act.wait_ge(ring_ready, z_item(i, half, c) + 1)
                    after(act, gated, CT * (2 * i + half - 2) + c + 1)
                    act.activation(gate[:, half, c, :], ring[:, j % 2, :], ACT.Silu).then_inc(ring_read, 1)

            def group_rstds(i):
                act.wait_ge(group_var_ready, i + 1)
                act.activation(spread[:, :], group_ps, ACT.Ln, bias=t.gn_eps[0:MP, :]).then_inc(group_log, 1)
                act.wait_ge(group_log, i + 1)
                act.activation(group_rstd[:, :], spread[:, :], ACT.Exp, scale=-0.5).then_inc(group_rstd_ready, 1)

            def pad_image(i):
                for c in range(CT):
                    for half in range(2):
                        j = pad_item(0, c, half)
                        act.wait_ge(ring_ready, pad_item(i, c, half) + 1)
                        if c == TEN:
                            after(act, conv_ready, 2 * i)
                        else:
                            after(act, taps_done[c], len(TAPS) * i)
                        act.activation(pad[c][:, 1 + half * ROWS:1 + (half + 1) * ROWS, 1:1 + WW],
                                       ring[:, j % 2, :].rearrange("p (h w) -> p h w", w=WW), ACT.Identity,
                                       bias=t.b_in1[:, c:c + 1]).then_inc(ring_read, 1)

            def finish_conv(i, half):
                act.wait_ge(conv_ready, 2 * i + half + 1)
                after(act, ema_steps[1], (2 * CT + 1) * i - CT - 1)
                act.activation(y[:, i, TEN, rows(half), :], conv_ps[:, half, :, :], ACT.Copy).then_inc(conv_read, 1)
                act.activation(turned[:, TEN, :, rows(half)].rearrange("p w h -> p h w"), conv_ps[:, half, :, :], ACT.Copy
                               ).then_inc(conv_read, 1)

            def exchange(i, c):
                act.wait_ge(taps_done[c], len(TAPS) * (i + 1))
                after(act, ema_steps[1], (2 * CT + 1) * i - CT - 1)
                carry_waits_act()
                act.activation(turned[:, c, :, :].rearrange("p w h -> p h w"), y[:, i, c, :, :], ACT.Copy
                               ).then_inc(turned_ready, 1)

            def gate_part(j):
                for half in range(2):
                    squares(j, half, gate_n(j, half))
                    silu_z(j, half)
                load_exp_ln()
                for half in range(2):
                    reciprocal_std(gate_n(j, half))

            def turn(i, b, j):
                if j is not None:
                    gate_part(j)
                pad_image(i)
                if b is not None:
                    squares(b, 0, final_n(b, 0))
                finish_conv(i, 0)
                if b is not None:
                    squares(b, 1, final_n(b, 1))
                    reciprocal_std(final_n(b, 0))
                exchange(i, 0)
                finish_conv(i, 1)
                if b is not None:
                    reciprocal_std(final_n(b, 1))
                if j is not None:
                    group_rstds(j)
                exchange(i, 1)

            gate_part(0)
            group_rstds(0)
            act.wait_ge(borders, CT)
            turn(0, None, 1)
            with act.Fori(1, NB - 1) as i:
                turn(i, i - 1, i + 1)
            turn(NB - 1, NB - 2, None)
            for half in range(2):
                squares(NB - 1, half, final_n(NB - 1, half))
            for half in range(2):
                reciprocal_std(final_n(NB - 1, half))

        @block.tensor
        def _(pe):
            def mean(n, half):
                pe.wait_ge(sum_y_done, 2 * n + 2)
                after(pe, centred, n)
                pe.matmul(mean_ps[:, :], avg, sum_y[:, half, :], start=True, stop=True).then_inc(mean_ready, 1)

            def variance(n):
                pe.wait_ge(sum_square_done, 2 * n + 2)
                after(pe, log_done, n)
                pe.matmul(var_ps[:, :], avg, sum_square[:, :], start=True, stop=True).then_inc(var_ready, 1)

            def z(i, half, tiles):
                pe.wait_ge(xz_ready, MT * (i + 1))
                for c in tiles:
                    j = z_item(0, half, c)
                    after(pe, ring_read, z_item(i, half, c) - 1)
                    for k in range(MT):
                        last = pe.matmul(ring[:, j % 2, :], t.w_in0[:, k, DI + c * P:DI + (c + 1) * P], xz[:, k, cols(half)],
                                         start=(k == 0), stop=(k == MT - 1))
                    last.then_inc(ring_ready, 1)

            def project(b, half, n, w):
                after(pe, out_read, 2 * n)
                for m in range(MT):
                    for k in range(CT):
                        last = pe.matmul(out_ps[:, m, :], w[:, k, m * MP:(m + 1) * MP], part(b, half, k),
                                         start=(k == 0), stop=(k == CT - 1))
                last.then_inc(projected, 1)

            def project_gate(i, half):
                pe.wait_ge(gated, CT * (2 * i + half + 1))
                project(i, half, gate_n(i, half), t.w_out0)

            def project_final(b, half, n):
                pe.wait_ge(scaled, CT * (n + 1))
                project(b, half, n, t.w_out1)

            def group_sums(i):
                pe.wait_ge(channel_done, MT * (i + 1))
                after(pe, conv_read, 4 * i)
                pe.matmul(group_ps, t.group_avg, channel[:, :, 0], start=True, stop=True).then_inc(group_mean_ready, 1)
                pe.wait_ge(group_steps, 4 * i + 4)
                pe.matmul(group_ps, t.group_avg, spread[:, :], start=True, stop=True).then_inc(group_var_ready, 1)

            def project_local(i, c):
                pe.wait_ge(xn_ready, MT * (i + 1))
                for half in range(2):
                    j = pad_item(0, c, half)
                    pe.wait_ge(ring_read, pad_item(i, c, half) - 1)
                    for k in range(MT):
                        last = pe.matmul(ring[:, j % 2, :], t.w_in1[:, k, c * P:(c + 1) * P], xn[:, k, cols(half)],
                                         start=(k == 0), stop=(k == MT - 1))
                    last.then_inc(ring_ready, 1)

            def convolve(i, half, taps):
                if taps.start == 0:
                    pe.wait_ge(ring_read, pad_item(i, TEN, 1) + 1)
                    pe.wait_ge(group_log, i + 1)
                    after(pe, conv_read, 4 * i)
                for k in taps:
                    di, dj = TAPS[k]
                    last = pe.matmul(conv_ps[:, half, :, :], diag[:, k, :],
                                     pad[TEN][:, half * ROWS + di:(half + 1) * ROWS + di, dj:dj + WW],
                                     start=(k == 0), stop=(k == len(TAPS) - 1))
                if taps.stop == len(TAPS):
                    last.then_inc(conv_ready, 1)

            def norm_and_z(j):
                mean(gate_n(j, 0), 0)
                z(j, 0, (0, 1))
                mean(gate_n(j, 1), 1)
                z(j, 0, (2,))
                z(j, 1, (0, 1))
                variance(gate_n(j, 0))
                z(j, 1, (2,))
                variance(gate_n(j, 1))

            def turn(i, b, j):
                if j is not None:
                    norm_and_z(j)
                for c in range(CT):
                    project_local(i, c)
                if j is not None:
                    project_gate(j, 0)
                convolve(i, 0, range(0, 3))
                if j is not None:
                    project_gate(j, 1)
                convolve(i, 0, range(3, 9))
                if b is not None:
                    mean(final_n(b, 0), 0)
                convolve(i, 1, range(0, 2))
                if b is not None:
                    mean(final_n(b, 1), 1)
                convolve(i, 1, range(2, 5))
                if b is not None:
                    variance(final_n(b, 0))
                convolve(i, 1, range(5, 9))
                if b is not None:
                    variance(final_n(b, 1))
                    project_final(b, 0, final_n(b, 0))
                if j is not None:
                    group_sums(j)
                if b is not None:
                    project_final(b, 1, final_n(b, 1))

            for m in range(MT):
                for k in range(CT):
                    last = pe.matmul(out_ps[:, m, 0:1], t.w_out1[:, k, m * MP:(m + 1) * MP], t.beta1[:, k:k + 1],
                                     start=(k == 0), stop=(k == CT - 1))
            last.then_inc(shift_product, 1)
            pe.wait_ge(shift_ready, 1)
            norm_and_z(0)
            for half in range(2):
                project_gate(0, half)
            group_sums(0)
            pe.wait_ge(diags, len(TAPS))
            turn(0, None, 1)
            with pe.Fori(1, NB - 1) as i:
                turn(i, i - 1, i + 1)
            turn(NB - 1, NB - 2, None)
            last = NB - 1
            for half in range(2):
                mean(final_n(last, half), half)
            for half in range(2):
                variance(final_n(last, half))
            for half in range(2):
                project_final(last, half, final_n(last, half))

        @block.vector
        def _(dve):
            def normalise_for_z(b):
                if inner(b, (0,)):
                    dve.wait_ge(ring_ready, z_item(b - 1, 1, CT - 1) + 1)
                for k in range(MT):
                    dve.tensor_scalar(xz[:, k, :], x[:, k, b, :], t.gn_mean[:, k, bass.ds(b, 1)], t.gn_rstd[:, k, bass.ds(b, 1)],
                                      ALU.subtract, ALU.mult).then_inc(xz_ready, 1)

            def centre(b, half, n):
                dve.wait_ge(mean_ready, n + 1)
                dve.tensor_tensor(lines(b, half), lines(b, half), mean_ps[:, None, :].broadcast_to([P, CT, NX]), ALU.subtract
                                  ).then_inc(centred, 1)

            def scale(b, half, n, gamma):
                dve.wait_ge(rstd_ready, n + 1)
                for k in range(CT):
                    here = line(b, half, k)
                    dve.scalar_tensor_tensor(here, here, gamma[:, k:k + 1], rstd[:, :], ALU.mult, ALU.mult).then_inc(scaled, 1)

            def centre_gate(j, half):
                centre(j, half, gate_n(j, half))

            def centre_final(b, half):
                centre(b, half, final_n(b, half))

            def scale_final(b, half):
                scale(b, half, final_n(b, half), t.gamma1)

            def apply_gate(j, half):
                n = gate_n(j, half)
                scale(j, half, n, t.gamma0)
                for k in range(CT):
                    here = line(j, half, k)
                    dve.wait_ge(ring_read, z_item(j, half, k) + 1)
                    dve.wait_ge(scaled, CT * n + k + 1)
                    dve.scalar_tensor_tensor(here, here, t.beta0[:, k:k + 1], gate[:, half, k, :], ALU.add, ALU.mult).then_inc(gated, 1)

            def residual_gate(j, half):
                n = gate_n(j, half)
                here = x[:, :, j, cols(half)]
                dve.wait_ge(projected, n + 1)
                dve.tensor_tensor(here, out_ps[:, :, :], here, ALU.add).then_inc(out_read, 2)
                dve.wait_ge(out_read, 2 * n + 2)
                carry_waits_dve()
                for k in range(MT):
                    dve.bn_stats(stats[:, k, half, :], x[:, k, j, cols(half)]).then_inc(stats_done, 1)
                if half:
                    dve.wait_ge(stats_done, 2 * MT * (j + 1))
                    carry_waits_dve()
                    for k in range(MT):
                        dve.bn_aggr(channel[:, k, :], stats[:, k, :, :]).then_inc(channel_done, 1)

            def residual_final(b, half):
                dve.wait_ge(projected, final_n(b, half) + 1)
                for m in range(MT):
                    here = x[:, m, b, cols(half)]
                    dve.scalar_tensor_tensor(here, out_ps[:, m, :], shift[:, m:m + 1], here, ALU.add, ALU.add).then_inc(out_read, 1)

            def group_spread(i):
                dve.wait_ge(group_mean_ready, i + 1)
                dve.tensor_copy(group_mean[:, :], group_ps).then_inc(group_steps, 1)
                dve.wait_ge(group_steps, 4 * i + 1)
                dve.tensor_tensor(spread[:, :], channel[:, :, 0], group_mean[:, :], ALU.subtract).then_inc(group_steps, 1)
                dve.wait_ge(group_steps, 4 * i + 2)
                dve.tensor_tensor(spread[:, :], spread[:, :], spread[:, :], ALU.mult).then_inc(group_steps, 1)
                dve.wait_ge(group_steps, 4 * i + 3)
                dve.tensor_tensor(spread[:, :], spread[:, :], channel[:, :, 1], ALU.add).then_inc(group_steps, 1)

            def normalise_for_local(i):
                dve.wait_ge(group_rstd_ready, i + 1)
                if inner(i, (0,)):
                    dve.wait_ge(ring_ready, pad_item(i - 1, CT - 1, 1) + 1)
                for k in range(MT):
                    dve.tensor_scalar(xn[:, k, :], x[:, k, i, :], group_mean[:, k:k + 1], group_rstd[:, k:k + 1],
                                      ALU.subtract, ALU.mult).then_inc(xn_ready, 1)

            def convolve(i, c, taps):
                if taps.start == 0:
                    dve.wait_ge(ring_read, pad_item(i, c, 1) + 1)
                for k in taps:
                    di, dj = TAPS[k]
                    window, here = pad[c][:, di:di + HH, dj:dj + WW], y[:, i, c, :, :]
                    if k:
                        dve.wait_ge(taps_done[c], len(TAPS) * i + k)
                        dve.scalar_tensor_tensor(here, window, t.conv_w1[:, c, k:k + 1], here, ALU.mult, ALU.add
                                                 ).then_inc(taps_done[c], 1)
                    else:
                        dve.tensor_scalar(here, window, t.conv_w1[:, c, k:k + 1], None, ALU.mult).then_inc(taps_done[c], 1)

            zeros_first = factor.rearrange("p l i -> p (l i)")

            def ema_forward(b, axis):
                if axis == 0:
                    dve.wait_ge(conv_read, 4 * (b + 1))
                    for c in VEC:
                        dve.wait_ge(taps_done[c], len(TAPS) * (b + 1))
                else:
                    dve.wait_ge(turned_ready, len(VEC) * (b + 1))
                    for k in range(CT):
                        after(dve, mixed_columns[k], b)
                for k in range(CT):
                    source = y[:, b, k, :, :] if axis == 0 else turned[:, k, :, :]
                    dve.tensor_tensor_scan(ema[axis][:, k, :, :].rearrange("p l i -> p (l i)"), zeros_first,
                                           source.rearrange("p l i -> p (l i)"), 0.0, ALU.mult, ALU.add).then_inc(ema_steps[axis], 1)

            def ema_backward(b, axis):
                done = (2 * CT + 1) * b + CT
                dve.wait_ge(ema_steps[axis], done)
                last = ema[axis][:, :, :, WW - 1]
                dve.tensor_scalar(last, last, 1 / (1 - DECAY ** 2), None, ALU.mult).then_inc(ema_steps[axis], 1)
                dve.wait_ge(ema_steps[axis], done + 1)
                for k in range(CT):
                    line_back = ema[axis][:, k, :, :].rearrange("p l i -> p (l i)")[:, ::-1]
                    dve.tensor_tensor_scan(line_back, zeros_first, line_back, 0.0, ALU.mult, ALU.add).then_inc(ema_steps[axis], 1)

            def mix_rows(b):
                dve.wait_ge(ema_steps[0], (2 * CT + 1) * (b + 1))
                here = y[:, b, :, :, :].rearrange("p k h w -> p (k h w)")
                dve.scalar_tensor_tensor(here, here, MIX_X, ema[0][:, :, :, :].rearrange("p k h w -> p (k h w)"), ALU.mult, ALU.add
                                         ).then_inc(mixed_rows, 1)

            def turn(i, b, j):
                def gate_step(step, *args):
                    if j is not None:
                        step(j, *args)

                def final_step(step, *args):
                    if b is not None:
                        step(b, *args)

                normalise_for_local(i)
                gate_step(normalise_for_z)
                gate_step(centre_gate, 0)
                final_step(ema_forward, 0)
                gate_step(centre_gate, 1)
                final_step(ema_forward, 1)
                final_step(ema_backward, 0)
                gate_step(apply_gate, 0)
                final_step(ema_backward, 1)
                gate_step(apply_gate, 1)
                final_step(mix_rows)
                gate_step(residual_gate, 0)
                for c in VEC:
                    final_step(lambda b: mix_columns(dve, b, c))
                convolve(i, 0, range(0, 2))
                gate_step(residual_gate, 1)
                convolve(i, 0, range(2, 5))
                final_step(centre_final, 0)
                convolve(i, 0, range(5, 8))
                final_step(centre_final, 1)
                convolve(i, 0, range(8, 9))
                convolve(i, 1, range(0, 2))
                final_step(scale_final, 0)
                convolve(i, 1, range(2, 5))
                final_step(scale_final, 1)
                final_step(residual_final, 0)
                gate_step(group_spread)
                convolve(i, 1, range(5, 9))
                final_step(residual_final, 1)

            dve.memset(factor, DECAY).then_inc(factors, 1)
            dve.wait_ge(factors, 1)
            dve.memset(factor[:, :, 0], 0.0).then_inc(factors, 1)
            dve.wait_ge(factors, 2)
            dve.wait_ge(shift_product, 1)
            dve.tensor_tensor(shift[:, :], out_ps[:, :, 0], t.b_out1, ALU.add).then_inc(shift_ready, 1)
            dve.wait_ge(shift_ready, 1)
            dve.wait_ge(sems.x_again[0], 16)
            normalise_for_z(0)
            for half in range(2):
                centre_gate(0, half)
            for half in range(2):
                apply_gate(0, half)
            for half in range(2):
                residual_gate(0, half)
            group_spread(0)
            for b in range(1, NB):
                dve.wait_ge(sems.x_again[b], 16)
            turn(0, None, 1)
            with dve.Fori(1, NB - 1) as i:
                turn(i, i - 1, i + 1)
            turn(NB - 1, NB - 2, None)
            last = NB - 1
            for axis in range(2):
                ema_forward(last, axis)
            for axis in range(2):
                ema_backward(last, axis)
            mix_rows(last)
            for c in VEC:
                mix_columns(dve, last, c)
            for step in (centre_final, scale_final, residual_final):
                for half in range(2):
                    step(last, half)


def build(nc, d, out):
    with ExitStack() as ctx:
        sb = lambda name, shape, dt=F32: ctx.enter_context(nc.sbuf_tensor(name, shape, dt))
        sem = lambda name: ctx.enter_context(nc.semaphore(name))
        sems = Names()
        sems.x_in = [sem(f"x_in{b}") for b in range(NB)]
        sems.x_again = [sem(f"x_again{b}") for b in range(NB)]
        sems.params, sems.fills, sems.out_done = sem("params"), sem("fills"), sem("out_done")
        t = Names()
        t.inner_params = sb("inner_params", [P, sum(INNER.values())])
        t.model_params = sb("model_params", [MP, sum(MODEL.values())])
        t.w_dt = sb("w_dt", [RK, DI])
        t.avg_inner = sb("avg_inner", [P, P])
        t.gn_eps, t.half_log_guard = sb("gn_eps", [P, 1]), sb("half_log_guard", [P, 1])
        t.gn_mean, t.gn_rstd = sb("gn_mean", [MP, MT, NB]), sb("gn_rstd", [MP, MT, NB])
        inner, model = unpack(t.inner_params, INNER), unpack(t.model_params, MODEL)
        t.conv_w0, t.conv_w1, t.conv_b0 = inner["conv_w0"], inner["conv_w1"], inner["conv_b0"]
        t.w_x, t.a_log, t.b_dt, t.d_skip = inner["w_x"], inner["a_log"], inner["b_dt"], inner["d_skip"]
        t.w_out0, t.w_out1, t.b_in1, t.ident = inner["w_out0"], inner["w_out1"], inner["b_in1"], inner["ident"]
        t.gamma0, t.beta0, t.gamma1, t.beta1 = inner["gamma0"], inner["beta0"], inner["gamma1"], inner["beta1"]
        t.w_in0, t.w_in1, t.b_out1, t.group_avg = model["w_in0"], model["w_in1"], model["b_out1"], model["group_avg"]
        u = sb("u", [P, NB, CT, HH, WW])
        y = sb("y", [P, NB, CT, HH, WW])
        stages(nc, t, sems, d, out, u, y)


def stages(nc, t, sems, d, out, u, y):
    with nc.sbuf_tensor("xn0", [MP, MT, NB, PX], F32) as xn:
        t.x = xn
        load(nc, t, sems, d)
        group_norm(nc, t, "gn0", xn, xn)
        project_and_convolve(nc, t, "conv0", xn, t.w_in0, None, t.conv_w0, t.conv_b0, ACT.Silu, u)
    selective_scans(nc, t, u, y)
    gate_mix_and_project(nc, t, sems, d, out, y, u)


_SOURCES = {"conv_w0": "L0_conv_conv_w", "conv_w1": "L1_conv_conv_w", "w_x": "L0_conv_W_x", "a_log": "L0_conv_A_log",
            "w_out0": "L0_conv_W_out", "w_out1": "L1_conv_W_out", "conv_b0": "L0_conv_conv_b", "b_dt": "L0_conv_b_dt",
            "d_skip": "L0_conv_D_param", "gamma0": "L0_conv_gamma", "beta0": "L0_conv_beta", "b_in1": "L1_conv_b_in",
            "gamma1": "L1_conv_ln_g", "beta1": "L1_conv_ln_b", "w_in0": "L0_conv_W_in", "w_in1": "L1_conv_W_in",
            "b_out1": "L1_conv_b_out"}


def kernel(**inputs):
    import numpy as np
    import concourse.bacc as bacc
    from concourse.bass_utils import run_bass_kernel_spmd as run

    nc = bacc.Bacc("TRN2", target_bir_lowering=False, num_devices=1)
    fixed = {"ident": np.eye(P, dtype=np.float32),
             "group_avg": np.kron(np.eye(MP // 6, dtype=np.float32), np.full((6, 6), 1 / 6, np.float32))}

    def pack(columns, rows):
        parts = [fixed[n] if n in fixed else
                 inputs[_SOURCES[n]].reshape(inputs[_SOURCES[n]].shape[0] // rows, rows, -1).transpose(1, 0, 2).reshape(rows, w)
                 for n, w in columns.items()]
        return np.ascontiguousarray(np.concatenate(parts, axis=1))

    arrays = {"x": np.ascontiguousarray(inputs["x"].reshape(NPOS, DM).T), "w_dt": np.ascontiguousarray(inputs["L0_conv_W_dt"]),
              "inner_params": pack(INNER, P), "model_params": pack(MODEL, MP)}
    maps, d = {}, {}
    for name, a in arrays.items():
        maps[f"in_{name}"] = a
        d[name] = nc.dram_tensor(f"in_{name}", a.shape, F32, kind="ExternalInput").ap()
    out = nc.dram_tensor("out", (DM, NPOS), F32, kind="ExternalOutput").ap()
    build(nc, d, out)
    r = run(nc, [maps], core_ids=[0])
    return np.ascontiguousarray(r.results[0]["out"].T).reshape(NB, HH, WW, DM)
```

```python
from contextlib import ExitStack

import concourse.bass as bass
from concourse import mybir

F32 = mybir.dt.float32
I32 = mybir.dt.int32
ALU = mybir.AluOpType
ACT = mybir.ActivationFunctionType
AX = mybir.AxisListType

NB, HH, WW, DM = 4, 32, 32, 192
DI, NS, RK = 384, 16, 12
PX = HH * WW
NPOS = NB * PX
P = 128
CT = DI // P
MP, MT = 96, DM // 96
NX = 512
HP, WP = HH + 2, WW + 2
XD = RK + 2 * NS
GN_EPS, LN_EPS = 1e-5, 1e-5
DECAY, GAIN = 0.6, 0.4
TC = 32
NDIR = 4
SEG = NDIR * NB
SW = TC + 2
FORWARD, BY_ROW = (0, 1), (0, 2)
SETUP = 7
GUARD = 1e-12
HALF_LOG_GUARD = 13.815510557964274
CHUNK_GROUP = 4
SQRT, EXP_AND_LN, SILU = 3, 6, 18
DEAD = -104.0


class Names:
    pass


INNER = {"conv_w0": CT * 9, "conv_w1": CT * 9, "w_x": CT * XD, "a_log": CT * NS, "w_out0": CT * DM, "w_out1": CT * DM,
         "conv_b0": CT, "b_dt": CT, "d_skip": CT, "gamma0": CT, "beta0": CT, "b_in1": CT, "gamma1": CT, "beta1": CT,
         "ident": P}
MODEL = {"w_in0": MT * 2 * DI, "w_in1": MT * DI, "b_out1": MT, "group_avg": MP}


def unpack(packed, columns):
    parts, at = {}, 0
    for name, n in columns.items():
        tiles = 1 if name in ("ident", "group_avg") else CT if columns is INNER else MT
        part = packed[:, at:at + n]
        parts[name] = part if tiles == 1 or n == tiles else part.rearrange("p (t n) -> p t n", t=tiles)
        at += n
    return parts


def settle(eng, semaphore, count):
    eng.wait_ge(semaphore, 1)
    eng.wait_ge(semaphore, count)


def after(eng, semaphore, count):
    if not isinstance(count, int) or count > 0:
        eng.wait_ge(semaphore, count)


def wait_carriers(nc, t, spare):
    places = iter(range(spare.shape[-1]))

    def free_place():
        place = next(places)
        return spare[:, place:place + 1]

    one = t.gn_eps[0:1, 0:1]
    return (lambda: nc.vector.memset(free_place(), 0.0),
            lambda: nc.scalar.activation(free_place(), one, ACT.Copy),
            lambda: nc.gpsimd.tensor_tensor(free_place(), one, one, ALU.mult))


def load_normalise_and_convolve(nc, t, sems, d, x, dst):
    VEC, TEN = (0, 1), 2
    ORDER = (0, TEN, 1)
    TAPS = [(i, j) for i in range(3) for j in range(3)]
    ROWS = HH // 2
    ITEMS, RING = 2 * CT, 3
    with ExitStack() as ctx:
        sem = lambda what: ctx.enter_context(nc.semaphore(f"c_{what}"))
        sb = lambda what, shape: ctx.enter_context(nc.sbuf_tensor(f"c_{what}", shape, F32))
        psum = lambda what, shape: ctx.enter_context(nc.psum_tensor(f"c_{what}", shape, F32))
        pad = [sb(f"pad{c}", [P, HP, WP]) for c in range(CT)]
        diag = sb("diag", [P, len(TAPS), P])
        stats, channel, group_mean = sb("stats", [MP, MT, 2, 6]), sb("channel", [MP, MT, 2]), sb("group_mean", [MP, MT])
        spread, std, rstd, offset = (sb(what, [MP, MT]) for what in ("spread", "std", "rstd", "offset"))
        spare = sb("spare", [1, 32])
        ring, conv_ps, group_ps = psum("ring", [P, RING, NX]), psum("conv", [P, 2, ROWS, WW]), psum("group", [MP, MT])
        borders, diags, stats_done, channel_done = sem("borders"), sem("diags"), sem("stats_done"), sem("channel_done")
        group_mean_ready, group_steps, group_var_ready, std_ready, offset_steps, normed = (
            sem("group_mean_ready"), sem("group_steps"), sem("group_var_ready"), sem("std_ready"), sem("offset_steps"), sem("normed"))
        ring_ready, ring_read, conv_ready, finished = sem("ring_ready"), sem("ring_read"), sem("conv_ready"), sem("finished")
        taps_done = [sem(f"taps_done{c}") for c in VEC]
        block = ctx.enter_context(nc.Block())
        carry_waits_dve, carry_waits_act, carry_waits_pool = wait_carriers(nc, t, spare)
        inner_loaded, model_loaded, w_dt_loaded = sems.params

        cols = lambda half: slice(half * NX, (half + 1) * NX)
        item = lambda b, c, half: ITEMS * b + 2 * ORDER.index(c) + half

        @block.sync
        def _(sp):
            for b in range(NB):
                sp.dma_start(x[:, :, b, :], d["x"].rearrange("(k p) (b n) -> p k b n", p=MP, b=NB)[:, :, b, :]
                             ).then_inc(sems.x_in[b], 16)

        @block.gpsimd
        def _(pool):
            pool.memset(t.gn_eps[:, :], GN_EPS).then_inc(sems.fills, 1)
            pool.memset(t.avg_inner[:, :], 1.0 / DI).then_inc(sems.fills, 1)
            pool.memset(t.half_log_guard[:, :], HALF_LOG_GUARD).then_inc(sems.fills, 1)
            for c in ORDER:
                pool.memset(pad[c][:, :, :], 0.0).then_inc(borders, 1)
            pool.wait_ge(inner_loaded, 16)
            for k in range(len(TAPS)):
                pool.tensor_scalar(diag[:, k, :], t.ident[:, :], t.conv_w0[:, TEN, k:k + 1], None, ALU.mult).then_inc(diags, 1)
            pool.tensor_scalar(t.conv_w1, t.conv_w1, GAIN / 4 * (1 - DECAY ** 2), 1.0, ALU.mult, ALU.mult).then_inc(sems.fills, 1)
            pool.wait_ge(sems.fills, 4)

        @block.tensor
        def _(pe):
            def group_means(b):
                pe.wait_ge(channel_done, MT * (b + 1))
                after(pe, std_ready, b)
                pe.matmul(group_ps[:, :], t.group_avg, channel[:, :, 0], start=True, stop=True).then_inc(group_mean_ready, 1)

            def group_variances(b):
                pe.wait_ge(group_steps, 4 * b + 4)
                pe.matmul(group_ps[:, :], t.group_avg, spread[:, :], start=True, stop=True).then_inc(group_var_ready, 1)

            def project(b):
                pe.wait_ge(normed, MT * (b + 1))
                for c in ORDER:
                    for half in range(2):
                        place = item(0, c, half) % RING
                        after(pe, ring_read, item(b, c, half) - RING + 1)
                        for k in range(MT):
                            last = pe.matmul(ring[:, place, :], t.w_in0[:, k, c * P:(c + 1) * P], x[:, k, b, cols(half)],
                                             start=(k == 0), stop=(k == MT - 1))
                        last.then_inc(ring_ready, 1)

            def convolve(b, half):
                if half == 0:
                    pe.wait_ge(ring_read, item(b, TEN, 1) + 1)
                    after(pe, finished, b)
                    if isinstance(b, int) and b == 0:
                        pe.wait_ge(diags, len(TAPS))
                for k, (i, j) in enumerate(TAPS):
                    last = pe.matmul(conv_ps[:, half, :, :], diag[:, k, :],
                                     pad[TEN][:, half * ROWS + i:(half + 1) * ROWS + i, j:j + WW],
                                     start=(k == 0), stop=(k == len(TAPS) - 1))
                last.then_inc(conv_ready, 1)

            def turn(b, ahead):
                project(b)
                if ahead is not None:
                    group_means(ahead)
                convolve(b, 0)
                if ahead is not None:
                    group_variances(ahead)
                convolve(b, 1)

            pe.wait_ge(model_loaded, 16)
            group_means(0)
            group_variances(0)
            turn(0, 1)
            with pe.Fori(1, NB - 1) as b:
                turn(b, b + 1)
            turn(NB - 1, None)

        @block.vector
        def _(dve):
            def channel_statistics(b):
                if isinstance(b, int) and b:
                    dve.wait_ge(group_steps, 4 * b)
                for k in range(MT):
                    for half in range(2):
                        dve.bn_stats(stats[:, k, half, :], x[:, k, b, cols(half)]).then_inc(stats_done, 1)
                dve.wait_ge(stats_done, 2 * MT * (b + 1))
                carry_waits_dve()
                for k in range(MT):
                    dve.bn_aggr(channel[:, k, :], stats[:, k, :, :]).then_inc(channel_done, 1)

            def group_spread(b):
                dve.wait_ge(group_mean_ready, b + 1)
                dve.tensor_copy(group_mean[:, :], group_ps[:, :]).then_inc(group_steps, 1)
                dve.wait_ge(group_steps, 4 * b + 1)
                dve.tensor_tensor(spread[:, :], channel[:, :, 0], group_mean[:, :], ALU.subtract).then_inc(group_steps, 1)
                dve.wait_ge(group_steps, 4 * b + 2)
                dve.tensor_tensor(spread[:, :], spread[:, :], spread[:, :], ALU.mult).then_inc(group_steps, 1)
                dve.wait_ge(group_steps, 4 * b + 3)
                dve.tensor_tensor(spread[:, :], spread[:, :], channel[:, :, 1], ALU.add).then_inc(group_steps, 1)

            def group_rstds(b):
                dve.wait_ge(std_ready, b + 1)
                after(dve, normed, MT * b)
                carry_waits_dve()
                dve.reciprocal(rstd[:, :], std[:, :]).then_inc(offset_steps, 1)
                dve.wait_ge(offset_steps, 2 * b + 1)
                dve.scalar_tensor_tensor(offset[:, :], group_mean[:, :], -1.0, rstd[:, :], ALU.mult, ALU.mult).then_inc(offset_steps, 1)
                for kept, value in ((t.gn_mean, group_mean), (t.gn_rstd, rstd)):
                    dve.tensor_copy(kept[:, :, bass.ds(b, 1)], value[:, :, None])

            def convolve(b, c, taps):
                if taps.start == 0:
                    dve.wait_ge(ring_read, item(b, c, 1) + 1)
                for k in taps:
                    (i, j) = TAPS[k]
                    window, out = pad[c][:, i:i + HH, j:j + WW], dst[:, b, c, :, :]
                    if k:
                        dve.wait_ge(taps_done[c], b * len(TAPS) + k)
                        dve.scalar_tensor_tensor(out, window, t.conv_w0[:, c, k:k + 1], out, ALU.mult, ALU.add
                                                 ).then_inc(taps_done[c], 1)
                    else:
                        dve.tensor_scalar(out, window, t.conv_w0[:, c, k:k + 1], t.conv_b0[:, c:c + 1], ALU.mult, ALU.add
                                          ).then_inc(taps_done[c], 1)

            def turn(b, ahead):
                convolve(b, 0, range(0, 1))
                if ahead is not None:
                    channel_statistics(ahead)
                convolve(b, 0, range(1, 5))
                if ahead is not None:
                    group_spread(ahead)
                convolve(b, 0, range(5, 9))
                convolve(b, 1, range(0, 2))
                if ahead is not None:
                    group_rstds(ahead)
                convolve(b, 1, range(2, 9))

            dve.wait_ge(sems.x_in[0], 16)
            channel_statistics(0)
            group_spread(0)
            group_rstds(0)
            dve.wait_ge(inner_loaded, 16)
            dve.wait_ge(sems.x_in[1], 16)
            turn(0, 1)
            for b in range(2, NB):
                dve.wait_ge(sems.x_in[b], 16)
            with dve.Fori(1, NB - 1) as b:
                turn(b, b + 1)
            turn(NB - 1, None)

        @block.scalar
        def _(act):
            def load_tables(which):
                act.add_instruction(mybir.InstLoadActFuncSet(name=nc.get_next_instruction_name(), act_func_set_id=which))

            def group_stds(b):
                load_tables(SQRT)
                act.wait_ge(group_var_ready, b + 1)
                act.activation(std[:, :], group_ps[:, :], ACT.Sqrt, bias=t.gn_eps[0:MP, :]).then_inc(std_ready, 1)
                load_tables(SILU)

            def normalise(b):
                act.wait_ge(offset_steps, 2 * b + 2)
                carry_waits_act()
                for k in range(MT):
                    act.activation(x[:, k, b, :], x[:, k, b, :], ACT.Identity, bias=offset[:, k:k + 1], scale=rstd[:, k:k + 1]
                                   ).then_inc(normed, 1)

            def pad_image(b, c):
                for half in range(2):
                    place = item(0, c, half) % RING
                    act.wait_ge(ring_ready, item(b, c, half) + 1)
                    if half == 0:
                        if c == TEN:
                            after(act, conv_ready, 2 * b)
                        else:
                            after(act, taps_done[c], b * len(TAPS))
                    act.activation(pad[c][:, 1 + half * ROWS:1 + (half + 1) * ROWS, 1:1 + WW],
                                   ring[:, place, :].rearrange("p (h w) -> p h w", w=WW), ACT.Copy).then_inc(ring_read, 1)

            def finish(b, c):
                out = dst[:, b, c, :, :]
                if c == TEN:
                    act.wait_ge(conv_ready, 2 * b + 2)
                    carry_waits_act()
                    act.activation(out, conv_ps[:, :, :, :].rearrange("p a h w -> p (a h) w"), ACT.Silu, bias=t.conv_b0[:, c:c + 1]
                                   ).then_inc(finished, 1)
                else:
                    act.wait_ge(taps_done[c], (b + 1) * len(TAPS))
                    carry_waits_act()
                    act.activation(out, out, ACT.Silu)

            def turn(b, ahead):
                if ahead is not None:
                    group_stds(ahead)
                finish(b, 0)
                if ahead is not None:
                    normalise(ahead)
                finish(b, TEN)
                if ahead is not None:
                    pad_image(ahead, 0)
                    pad_image(ahead, TEN)
                finish(b, 1)
                if ahead is not None:
                    pad_image(ahead, 1)

            for place, name, loaded in ((t.model_params, "model_params", model_loaded), (t.inner_params, "inner_params", inner_loaded),
                                        (t.w_dt, "w_dt", w_dt_loaded)):
                act.dma_start(place[:, :], d[name]).then_inc(loaded, 16)
            act.wait_ge(sems.fills, 1)
            group_stds(0)
            normalise(0)
            act.wait_ge(normed, MT)
            act.activation(t.xz[:, :, :], x[:, :, 0, :], ACT.Copy)
            for place, c in enumerate(ORDER):
                act.wait_ge(borders, place + 1)
                pad_image(0, c)
            turn(0, 1)
            with act.Fori(1, NB - 1) as b:
                turn(b, b + 1)
            turn(NB - 1, None)
            act.wait_ge(w_dt_loaded, 16)


def selective_scans(nc, t, u, y):
    with ExitStack() as ctx:
        sem = lambda what: ctx.enter_context(nc.semaphore(f"ssm_{what}"))
        sb = lambda what, shape, dt=F32: ctx.enter_context(nc.sbuf_tensor(f"ssm_{what}", shape, dt))
        a_neg = sb("a_neg", [P, CT, NS])
        a_half = sb("a_half", [P, CT, NS])
        a_slow = sb("a_slow", [P, 2, CT])
        d_skip4 = sb("d_skip4", [P, CT])
        half_ident = sb("half_ident", [P, P])
        seg_mask = sb("seg_mask", [P, SEG, SW])
        carry = sb("carry", [P, NS, CT, SEG])
        xd = sb("xd", [XD, SEG * TC])
        dt = sb("dt", [P, CT, SEG, SW])
        cum = sb("cum", [P, CT, SEG, SW])
        dtu = sb("dtu", [P, CT, SEG, TC])
        gate = sb("gate", [P, CT, SEG, TC])
        decay = sb("decay", [P, CT, SEG, SW])
        drive = sb("drive", [P, CT, SEG, SW])
        h = sb("h", [P, CT, SEG, SW])
        hc = sb("hc", [P, CT, SEG, TC])
        min_cum = sb("min_cum", [P, CT])
        slowest = sb("slowest", [P, 2, CT])
        score = sb("score", [P, 2])
        top = sb("top", [1, 2])
        spare, carriers = sb("spare", [1, 2]), sb("carriers", [1, 32])
        flags = sb("flags", [1, 2], I32)
        ps_y = ctx.enter_context(nc.psum_tensor("ssm_ps_y", [P, CT, SEG, TC], F32))
        ps_bc = ctx.enter_context(nc.psum_tensor("ssm_ps_bc", [P, 2, 2, SEG, TC], F32))
        ps_x = ctx.enter_context(nc.psum_tensor("ssm_ps_x", [P, SEG * TC], F32))

        y_init, setup, a_exp, a_steps = sem("y_init"), sem("setup"), sem("a_exp"), sem("a_steps")
        xdbl_ready, xd_copied, pre_ready = sem("xdbl_ready"), sem("xd_copied"), sem("pre_ready")
        abs_done, exp_done, ln_done = sem("abs_done"), sem("exp_done"), sem("ln_done")
        clipped, entered, rounded, corrected, log_added, dt_ready, cum_ready, dtu_ready = (
            sem("clipped"), sem("entered"), sem("rounded"), sem("corrected"), sem("log_added"), sem("dt_ready"), sem("cum_ready"),
            [sem(f"dtu_ready{k}") for k in range(CT)])
        score_steps, score_ready, score_rows = sem("score_steps"), sem("score_ready"), sem("score_rows")
        top_ready, flags_ready, added = sem("top_ready"), sem("flags_ready"), sem("added")
        pair = lambda what: [[sem(f"{what}{g}{c}") for c in range(CT)] for g in range(2)]
        bc_ready = [sem("bc_ready0"), sem("bc_ready1")]
        tanh_done, gate_ready, gated = pair("tanh_done"), pair("gate_ready"), pair("gated")
        driven, scanned, hc_ready, summed = pair("driven"), pair("scanned"), pair("hc_ready"), pair("summed")
        saved = pair("saved")
        block = ctx.enter_context(nc.Block())
        _, _, carry_waits_pool = wait_carriers(nc, t, carriers)

        def along(v, c, direction, k=slice(None)):
            v = v[:, :, :, :, :].rearrange("p b k h w -> p k b h w")
            i = c if direction in FORWARD else HH - 1 - c
            return v[:, k, :, i, :] if direction in BY_ROW else v[:, k, :, :, i]

        def at_ends(v, k, forward, backward):
            whole = v[:, :, :, :]
            (parts, tile, seg) = whole.ap[0], whole.ap[1], whole.ap[2]
            tiles = [[tile[0], len(k)]] if len(k) > 1 else []
            return bass.AP(tensor=whole.tensor, offset=whole.offset + k[0] * tile[0] + forward,
                           ap=[parts, *tiles, [seg[0] * SEG // 2 + backward - forward, 2], [seg[0], SEG // 2]])

        START, END = (0, SW - 1), (TC, 1)
        halves = lambda v: v.rearrange("p (f s) -> p f s", f=2)

        segs = lambda direction: slice(direction * NB, (direction + 1) * NB)
        before = lambda c, n: c * (NS - 1) + n - 1

        def chunks(eng, work, rest, close):
            live = [eng.alloc_register(f"live_any_{eng.engine}"), eng.alloc_register(f"live_rest_{eng.engine}")]
            for reg in live:
                eng.reg_mov(reg, 1)
            with eng.Fori(0, 2) as part:
                with eng.If_ne(live[0], 0):
                    with eng.Fori(0, HH // CHUNK_GROUP // 2) as group:
                        with eng.If_ne(live[0], 0):
                            with eng.Fori(0, CHUNK_GROUP) as i:
                                c = part * (HH // 2) + group * CHUNK_GROUP + i
                                with eng.If_ne(live[0], 0):
                                    work(c)
                                    with eng.If_ne(live[1], 0):
                                        rest(c)
                                    close(c)
                                    settle(eng, flags_ready, c + 1)
                                    for j, reg in enumerate(live):
                                        eng.reg_load(reg, flags[0:1, j:j + 1])
                                eng.nop()
                        eng.nop()
                eng.nop()

        def states(eng, unit):
            with eng.Fori(1, NS - 1, 2) as n:
                unit(n, 1)
                unit(n + 1, 0)
            unit(NS - 1, 1)

        def weigh_by_u(eng, c, k):
            for r in range(NDIR):
                eng.tensor_tensor(dtu[:, k, segs(r), :], dt[:, k, segs(r), 1:1 + TC], along(u, c, r, k), ALU.mult
                                  ).then_inc(dtu_ready[k], 1)

        @block.gpsimd
        def _(pool):
            for k in range(CT):
                pool.wait_ge(a_steps, 1)
                pool.tensor_scalar(y[:, :, k, :, :], u[:, :, k, :, :], d_skip4[:, k:k + 1], 1.0, ALU.mult, ALU.mult
                                   ).then_inc(y_init, 1)

            def unit_tile(k, n, g, count):
                pool.wait_ge(gate_ready[g][k], count + 1)
                pool.tensor_tensor(gate[:, k, :, :], gate[:, k, :, :], dtu[:, k, :, :], ALU.mult).then_inc(gated[g][k], 1)
                if g:
                    pool.wait_ge(scanned[1][k], 2 * count + 1)
                pool.tensor_tensor(at_ends(drive, [k], *START), halves(carry[:, n, k, :]), halves(seg_mask[:, :, 1]), ALU.mult
                                   ).then_inc(gated[g][k], 1)

            def unit(c, n, g, count):
                for k in range(CT):
                    unit_tile(k, n, g, count)

            def work(c):
                for k in range(CT):
                    pool.wait_ge(rounded, CT * c + k + 1)
                    pool.tensor_tensor(drive[:, k, :, 1:1 + TC], gate[:, k, :, :], drive[:, k, :, 1:1 + TC], ALU.subtract
                                       ).then_inc(corrected, 1)

                for k in (0, 1):
                    pool.wait_ge(dt_ready, CT * c + k + 1)
                    carry_waits_pool()
                    weigh_by_u(pool, c, k)
                for k in range(CT):
                    pool.wait_ge(dtu_ready[k], NDIR * (c + 1))
                    unit_tile(k, 0, 0, c)

            def rest(c):
                for k in range(CT):
                    pool.wait_ge(scanned[0][k], 2 * c + 2)
                pool.tensor_tensor(spare[:, 1:2], seg_mask[0:1, 0, 0:1], seg_mask[0:1, 0, 0:1], ALU.mult)
                states(pool, lambda n, parity: unit(c, n, 1, before(c, n)))

            chunks(pool, work, rest, lambda c: None)

        @block.scalar
        def _(act):
            act.activation(a_neg[:, :, :], t.a_log, ACT.Exp).then_inc(a_exp, 1)

            def unit_tile(k, n, g, count):
                if g:
                    act.wait_ge(driven[1][k], count + 1)
                act.activation(gate[:, k, :, :], cum[:, k, :, 1:1 + TC], ACT.Tanh, bias=t.half_log_guard[:, :],
                               scale=a_half[:, k, bass.ds(n, 1)]).then_inc(tanh_done[g][k], 1)
                if g:
                    act.wait_ge(scanned[1][k], 2 * count + 1)
                act.activation(decay[:, k, :, 1:1 + TC], dt[:, k, :, 1:1 + TC], ACT.Exp, scale=a_neg[:, k, bass.ds(n, 1)])
                act.wait_ge(tanh_done[g][k], count + 1)
                act.activation(gate[:, k, :, :], gate[:, k, :, :], ACT.Identity, bias=1.0).then_inc(gate_ready[g][k], 1)

            def unit(n, g, count):
                for k in range(CT):
                    unit_tile(k, n, g, count)

            def work(c):
                act.wait_ge(xdbl_ready, c + 1)
                act.activation(xd[:, :], ps_x[0:XD, :], ACT.Copy).then_inc(xd_copied, 1)
                for k in range(CT):
                    act.wait_ge(pre_ready, CT * c + k + 1)
                    act.activation(gate[:, k, :, :], ps_y[:, k, :, :], ACT.Abs, bias=t.b_dt[:, k:k + 1]).then_inc(abs_done, 1)
                for k in range(CT):
                    act.wait_ge(abs_done, CT * c + k + 1)
                    act.activation(gate[:, k, :, :], gate[:, k, :, :], ACT.Exp, scale=-1.0).then_inc(exp_done, 1)
                for k in range(CT):
                    act.wait_ge(exp_done, CT * c + k + 1)
                    act.activation(dtu[:, k, :, :], gate[:, k, :, :], ACT.Ln, bias=1.0).then_inc(ln_done, 1)
                act.wait_ge(a_steps, 3)
                for k in range(CT):
                    act.wait_ge(corrected, CT * c + k + 1)
                    act.wait_ge(cum_ready, 2 * (CT * c + k + 1))
                    unit_tile(k, 0, 0, c)

            def rest(c):
                for k in range(CT):
                    act.wait_ge(scanned[0][k], 2 * c + 2)
                states(act, lambda n, parity: unit(n, 1, before(c, n)))

            chunks(act, work, rest, lambda c: None)

        @block.tensor
        def _(pe):
            for s in (*driven[1], *scanned[1], *summed[1], added):
                pe.sem_inc(s, 1)

            def spread(n, parity, g):
                for j in range(2):
                    row = RK + j * NS + n
                    last = pe.matmul(ps_bc[:, parity, j, :, :], t.ident[0:XD, row:row + 1].broadcast_to([XD, P]), xd[:, :],
                                     start=True, stop=True)
                last.then_inc(bc_ready[g], 1)

            def add_up(g, count):
                for k in range(CT):
                    pe.wait_ge(hc_ready[g][k], count + 1)
                    pe.matmul(ps_y[:, k, :, :], half_ident[:, :], hc[:, k, :, :], start=(g == 0), stop=(g == 0),
                              skip_group_check=True).then_inc(summed[g][k], 1)

            def work(c):
                for r in range(NDIR):
                    for k in range(CT):
                        last = pe.matmul(ps_x[0:XD, r * NB * TC:(r + 1) * NB * TC], t.w_x[:, k, :], along(u, c, r, k),
                                         start=(k == 0), stop=(k == CT - 1))
                last.then_inc(xdbl_ready, 1)
                pe.wait_ge(xd_copied, c + 1)
                pe.wait_ge(added, NDIR * c + 1)
                for k in range(CT):
                    pe.matmul(ps_y[:, k, :, :], t.w_dt[:, k * P:(k + 1) * P], xd[0:RK, :], start=True, stop=True
                              ).then_inc(pre_ready, 1)
                spread(0, 0, 0)
                pe.wait_ge(setup, SETUP)
                pe.wait_ge(score_ready, c + 1)
                for j in range(2):
                    last = pe.matmul(ps_x[0:1, j * P:(j + 1) * P], score[:, j:j + 1], t.ident, start=True, stop=True)
                last.then_inc(score_rows, 1)
                add_up(0, c)

            def rest(c):
                spread(1, 1, 1)
                for n in range(1, NS):
                    if n + 1 < NS:
                        spread(n + 1, (n + 1) % 2, 1)
                    add_up(1, before(c, n))

            chunks(pe, work, rest, lambda c: None)

        @block.vector
        def _(dve):
            dve.tensor_scalar(d_skip4[:, :], t.d_skip, float(NDIR), None, ALU.mult).then_inc(a_steps, 1)
            dve.wait_ge(a_exp, 1)
            dve.tensor_scalar(a_half[:, :, :], a_neg[:, :, :], -0.5, None, ALU.mult).then_inc(a_steps, 1)
            dve.wait_ge(a_steps, 2)
            dve.tensor_scalar(a_neg[:, :, :], a_neg[:, :, :], -1.0, None, ALU.mult).then_inc(a_steps, 1)
            dve.wait_ge(a_steps, 3)
            dve.tensor_reduce(a_slow[:, 0, :], a_neg[:, :, :], AX.X, ALU.max).then_inc(a_steps, 1)
            dve.tensor_reduce(a_slow[:, 1, :], a_neg[:, :, 1:], AX.X, ALU.max).then_inc(a_steps, 1)
            dve.memset(seg_mask[:, :, :], 1.0).then_inc(setup, 1)
            dve.memset(carry[:, :, :, :], 0.0).then_inc(setup, 1)
            for v in (decay, drive, dt):
                dve.memset(v[:, :, :, 0:SW:SW - 1], 0.0).then_inc(setup, 1)
            dve.memset(cum[:, :, :, 1:TC + 1:TC - 1], 0.0).then_inc(setup, 1)
            dve.tensor_scalar(half_ident[:, :], t.ident, 0.5, None, ALU.mult).then_inc(setup, 1)
            dve.wait_ge(setup, SETUP)
            for end in START:
                dve.memset(seg_mask[:, :, end], 0.0).then_inc(a_steps, 1)
            dve.wait_ge(a_steps, 7)

            def scan(out, factor, term, done):
                for part in (slice(0, SEG // 2), slice(SEG // 2, SEG)):
                    lines = [v[:, part, :].rearrange("p s w -> p (s w)") for v in (out, factor, term)]
                    if part.start:
                        lines = [v[:, ::-1] for v in lines]
                    dve.tensor_tensor_scan(*lines, 0.0, ALU.mult, ALU.add).then_inc(done, 1)

            def unit(n, parity, g, count):
                def drive_tile(k):
                    if k == 0:
                        dve.wait_ge(bc_ready[g], count + 1)
                    dve.wait_ge(gated[g][k], 2 * count + 2)
                    dve.tensor_tensor(drive[:, k, :, 1:1 + TC], gate[:, k, :, :], ps_bc[:, parity, 0, :, :], ALU.mult
                                      ).then_inc(driven[g][k], 1)

                def scan_tile(k):
                    dve.wait_ge(driven[g][k], count + 1 + g)
                    scan(h[:, k, :, :], decay[:, k, :, :], drive[:, k, :, :], scanned[g][k])

                def weigh_tile(k):
                    dve.wait_ge(scanned[g][k], 2 * count + 2 + g)
                    if g:
                        dve.wait_ge(summed[1][k], count + 1)
                    dve.tensor_tensor(hc[:, k, :, :], h[:, k, :, 1:1 + TC], ps_bc[:, parity, 1, :, :], ALU.mult
                                      ).then_inc(hc_ready[g][k], 1)
                    dve.tensor_copy(halves(carry[:, n, k, :]), at_ends(h, [k], *END)).then_inc(saved[g][k], 1)

                drive_tile(0)
                if g:
                    drive_tile(1)
                    scan_tile(0)
                else:
                    scan_tile(0)
                    drive_tile(1)
                drive_tile(2)
                scan_tile(1)
                weigh_tile(0)
                scan_tile(2)
                weigh_tile(1)
                weigh_tile(2)

            def work(c):
                for k in range(CT):
                    dve.wait_ge(abs_done, CT * c + k + 1)
                    dve.tensor_scalar(dt[:, k, :, 1:1 + TC], ps_y[:, k, :, :], t.b_dt[:, k:k + 1], 0.0, ALU.add, ALU.max
                                      ).then_inc(clipped, 1)
                dve.tensor_copy(at_ends(dt, range(CT), *START), at_ends(cum, range(CT), *END)).then_inc(entered, 1)
                for k in range(CT):
                    dve.wait_ge(exp_done, CT * c + k + 1)
                    dve.tensor_scalar(drive[:, k, :, 1:1 + TC], gate[:, k, :, :], 1.0, -1.0, ALU.add, ALU.add).then_inc(rounded, 1)

                def add_log(k):
                    dve.wait_ge(ln_done, CT * c + k + 1)
                    dve.wait_ge(clipped, CT * c + k + 1)
                    dve.tensor_tensor(dt[:, k, :, 1:1 + TC], dt[:, k, :, 1:1 + TC], dtu[:, k, :, :], ALU.add).then_inc(log_added, 1)

                def add_correction(k):
                    dve.wait_ge(corrected, CT * c + k + 1)
                    dve.wait_ge(log_added, CT * c + k + 1)
                    dve.tensor_tensor(dt[:, k, :, 1:1 + TC], dt[:, k, :, 1:1 + TC], drive[:, k, :, 1:1 + TC], ALU.add).then_inc(dt_ready, 1)

                def accumulate(k):
                    dve.wait_ge(entered, c + 1)
                    dve.wait_ge(dt_ready, CT * c + k + 1)
                    scan(cum[:, k, :, :], seg_mask[:, :, :], dt[:, k, :, :], cum_ready)

                add_log(0)
                add_correction(0)
                add_log(1)
                accumulate(0)
                add_correction(1)
                add_log(2)
                accumulate(1)
                add_correction(2)
                accumulate(2)
                weigh_by_u(dve, c, 2)
                dve.wait_ge(cum_ready, 2 * CT * c + 2 * CT)
                dve.tensor_reduce(min_cum[:, :], at_ends(cum, range(CT), *END), AX.XY, ALU.min).then_inc(score_steps, 1)
                dve.wait_ge(score_steps, 3 * c + 1)
                for j in range(2):
                    dve.tensor_tensor(slowest[:, j, :], a_slow[:, j, :], min_cum[:, :], ALU.mult).then_inc(score_steps, 1)
                dve.wait_ge(score_steps, 3 * c + 3)
                dve.tensor_reduce(score[:, :], slowest[:, :, :], AX.X, ALU.max).then_inc(score_ready, 1)
                unit(0, 0, 0, c)
                dve.wait_ge(score_rows, c + 1)
                dve.tensor_reduce(top[:, :], ps_x[0:1, 0:2 * P].rearrange("p (j n) -> p j n", j=2), AX.X, ALU.max
                                  ).then_inc(top_ready, 1)
                dve.wait_ge(top_ready, c + 1)
                dve.tensor_scalar(flags[:, :], top[:, :], DEAD, None, ALU.is_gt).then_inc(flags_ready, 1)

            def rest(c):
                for k in range(CT):
                    settle(dve, summed[0][k], c + 1)
                states(dve, lambda n, parity: unit(n, parity, 1, before(c, n)))
                for k in range(CT):
                    dve.wait_ge(summed[1][k], before(c, NS) + 1)
                    dve.wait_ge(saved[1][k], before(c, NS))
                dve.memset(spare[:, 0:1], 0.0)

            def close(c):
                dve.wait_ge(y_init, CT)
                for k in range(CT):
                    settle(dve, summed[0][k], c + 1)
                    settle(dve, saved[0][k], c + 1)
                for place, r in enumerate(sorted(range(NDIR), key=lambda r: r not in BY_ROW)):
                    if place == NDIR // 2:
                        dve.wait_ge(added, NDIR * c + place + 1)
                        dve.memset(spare[:, 0:1], 0.0)
                    dve.tensor_tensor(along(y, c, r), ps_y[:, :, segs(r), :], along(y, c, r), ALU.add).then_inc(added, 1)

            chunks(dve, work, rest, close)



def gate_mix_and_project(nc, t, sems, d, out, y, u):
    VEC, TEN = (0, 1), 2
    TAPS = [(i, j) for i in range(3) for j in range(3)]
    ROWS = HH // 2
    ITEMS = 2 * CT
    MIX_X = (1 + GAIN / 2) / (GAIN / 4 * (1 - DECAY ** 2))
    with ExitStack() as ctx:
        sem = lambda what: ctx.enter_context(nc.semaphore(f"t_{what}"))
        sb = lambda what, shape: ctx.enter_context(nc.sbuf_tensor(f"t_{what}", shape, F32))
        psum = lambda what, shape: ctx.enter_context(nc.psum_tensor(f"t_{what}", shape, F32))
        whole_u = u[:, :, :, :, :].rearrange("p b k h w -> p (b k h w)")
        x = whole_u[0:MP, 0:MT * NPOS].rearrange("p (k b n) -> p k b n", k=MT, b=NB)
        turned = whole_u[:, MT * NPOS:MT * NPOS + CT * PX].rearrange("p (k w h) -> p k w h", k=CT, w=WW)
        factor = whole_u[:, MT * NPOS + CT * PX:].rearrange("p (l i) -> p l i", i=WW)
        xz, xn = t.xz, sb("xn", [MP, MT, PX])
        pad = [sb(f"pad{c}", [P, HP, WP]) for c in range(CT)]
        diag = sb("diag", [P, len(TAPS), P])
        square, gate = sb("square", [P, CT, NX]), sb("gate", [P, 2, CT, NX])
        sum_y, sum_square, rstd = sb("sum_y", [P, 2, NX]), sb("sum_square", [P, NX]), sb("rstd", [P, NX])
        ema = [sb("ema_w", [P, CT, HH, WW]), sb("ema_h", [P, CT, WW, HH])]
        stats, channel = sb("stats", [MP, MT, 2, 6]), sb("channel", [MP, MT, 2])
        group_mean, spread, group_rstd = sb("group_mean", [MP, MT]), sb("spread", [MP, MT]), sb("group_rstd", [MP, MT])
        shift, spare = sb("shift", [MP, MT]), sb("spare", [1, 64])
        mean_ps, var_ps = psum("mean_ps", [P, NX]), psum("var_ps", [P, NX])
        out_ps = psum("out_ps", [MP, MT, NX])
        ring = psum("ring", [P, 2, NX])
        conv_ps = psum("conv_ps", [P, 2, ROWS, WW])
        group_ps = conv_ps[0:MP, 0, 0, 0:MT]

        borders, diags, factors, shift_product, shift_ready = (
            sem("borders"), sem("diags"), sem("factors"), sem("shift_product"), sem("shift_ready"))
        sum_y_done, mean_ready, centred, squared = sem("sum_y_done"), sem("mean_ready"), sem("centred"), sem("squared")
        sum_square_done, var_ready, log_done, rstd_ready = (
            sem("sum_square_done"), sem("var_ready"), sem("log_done"), sem("rstd_ready"))
        scaled, gated, projected, out_read = sem("scaled"), sem("gated"), sem("projected"), sem("out_read")
        xz_ready, ring_ready, ring_read = sem("xz_ready"), sem("ring_ready"), sem("ring_read")
        stats_done, channel_done, group_steps = sem("stats_done"), sem("channel_done"), sem("group_steps")
        group_mean_ready, group_var_ready, group_log, group_rstd_ready = (
            sem("group_mean_ready"), sem("group_var_ready"), sem("group_log"), sem("group_rstd_ready"))
        xn_ready, centred_tiles, squared_tiles = sem("xn_ready"), sem("centred_tiles"), sem("squared_tiles")
        taps_done = [sem(f"taps_done{c}") for c in VEC]
        conv_ready, conv_read, turned_ready = sem("conv_ready"), sem("conv_read"), sem("turned_ready")
        ema_steps = [sem("ema_w_steps"), sem("ema_h_steps")]
        mixed_rows, mixed_columns = sem("mixed_rows"), [sem(f"mixed_columns{k}") for k in range(CT)]
        block = ctx.enter_context(nc.Block())

        avg, eps = t.avg_inner[:, :], t.gn_eps[:, :]
        cols = lambda half: slice(half * NX, (half + 1) * NX)
        rows = lambda half: slice(half * ROWS, (half + 1) * ROWS)
        part = lambda b, half, k=slice(None): y[:, b, k, rows(half), :]
        line = lambda b, half, k: part(b, half, k).rearrange("p h w -> p (h w)")
        lines = lambda b, half: part(b, half).rearrange("p k h w -> p k (h w)")

        end_mean = [conv_ps[:, half, :, :].rearrange("p h w -> p (h w)") for half in range(2)]
        end_square = lambda half, k: ema[0][:, k, rows(half), :].rearrange("p h w -> p (h w)")
        end_rstd = [ema[1][:, 0, rows(half), :].rearrange("p h w -> p (h w)") for half in range(2)]
        end_var = [mean_ps, var_ps]
        last_out = [out_ps[:, :, :], conv_ps[0:MP, :, :, :].rearrange("p a h w -> p a (h w)")]

        inner = lambda image, excepted: not isinstance(image, int) or image not in excepted

        def turn_item(i):
            return 2 * ITEMS * i + ITEMS

        def z_item(j, half, c):
            return turn_item(j - 1) + (ITEMS if isinstance(j, int) and j < 2 else 0) + half * CT + c

        def pad_item(i, c, half):
            return turn_item(i) + (ITEMS if inner(i, (0, NB - 1)) else 0) + 2 * c + half

        AHEAD = 2

        def gate_n(j, half):
            return (4 * j - 4 if inner(j, (0, 1)) else 2 * j) + half

        def final_n(b, half):
            return 4 * b + (6 if inner(b, (NB - 2, NB - 1)) else 4 if b == NB - 2 else 2) + half

        carry_waits_dve, carry_waits_act, carry_waits_pool = wait_carriers(nc, t, spare)

        def mix_columns(eng, b, k):
            eng.wait_ge(mixed_rows, b + 1)
            eng.wait_ge(ema_steps[1], (2 * CT + 1) * (b + 1))
            if eng is nc.gpsimd:
                carry_waits_pool()
            eng.tensor_tensor(y[:, b, k, :, :], y[:, b, k, :, :], ema[1][:, k, :, :].rearrange("p w h -> p h w"), ALU.add
                              ).then_inc(mixed_columns[k], 1)

        @block.sync
        def _(sp):
            for b in range(NB):
                sp.dma_start(x[:, :, b, :], d["x"].rearrange("(k p) (b n) -> p k b n", p=MP, b=NB)[:, :, b, :]
                             ).then_inc(sems.x_again[b], 16)
            for b in range(NB):
                sp.wait_ge(out_read, 2 * final_n(b, 1) + 2)
                sp.dma_start(out.rearrange("(k p) (b n) -> p k b n", p=MP, b=NB)[:, :, b, :], x[:, :, b, :]
                             ).then_inc(sems.out_done, 16)
            sp.wait_ge(sems.out_done, 16 * NB)

        @block.gpsimd
        def _(pool):
            def sums_of_tiles(b, half, n):
                after(pool, mean_ready, n - 1)
                carry_waits_pool()
                n, here = n - AHEAD, sum_y[:, half, :]
                pool.tensor_tensor(here, line(b, half, 0), line(b, half, 1), ALU.add).then_inc(sum_y_done, 1)
                pool.wait_ge(sum_y_done, 2 * n + 1)
                carry_waits_pool()
                pool.tensor_tensor(here, here, line(b, half, 2), ALU.add).then_inc(sum_y_done, 1)

            def sums_of_squares(n):
                after(pool, var_ready, n)
                n = n - AHEAD
                pool.wait_ge(squared, n + 1)
                pool.tensor_tensor(sum_square[:, :], square[:, 0, :], square[:, 1, :], ALU.add).then_inc(sum_square_done, 1)
                pool.wait_ge(sum_square_done, 2 * n + 1)
                pool.tensor_tensor(sum_square[:, :], sum_square[:, :], square[:, 2, :], ALU.add).then_inc(sum_square_done, 1)

            def norm(image, number):
                for half in range(2):
                    sums_of_tiles(image, half, number(image, half))
                for half in range(2):
                    sums_of_squares(number(image, half))

            def norm_of_mixed(b):
                mix_columns(pool, b, TEN)
                for c in range(CT):
                    pool.wait_ge(mixed_columns[c], b + 1)
                norm(b, final_n)

            norm(1, gate_n)
            for c in range(CT):
                pool.memset(pad[c][:, :, :], 0.0).then_inc(borders, 1)
            for k in range(len(TAPS)):
                pool.tensor_scalar(diag[:, k, :], t.ident, t.conv_w1[:, TEN, k:k + 1], 1.0, ALU.mult, ALU.mult).then_inc(diags, 1)
            with pool.Fori(1, NB - 1) as i:
                norm(i + 1, gate_n)
                norm_of_mixed(i - 1)
            norm_of_mixed(NB - 2)
            mix_columns(pool, NB - 1, TEN)

        @block.scalar
        def _(act):
            def load_tables(which):
                act.add_instruction(mybir.InstLoadActFuncSet(name=nc.get_next_instruction_name(), act_func_set_id=which))

            def squares(b, half, n):
                act.wait_ge(centred, n - AHEAD + 1)
                after(act, sum_square_done, 2 * (n - AHEAD))
                act.activation(square[:, :, :], lines(b, half), ACT.Square).then_inc(squared, 1)

            def reciprocal_std(n):
                act.wait_ge(var_ready, n + 1)
                after(act, scaled, CT * n)
                act.activation(rstd[:, :], var_ps[:, :], ACT.Ln, bias=eps).then_inc(log_done, 1)
                act.wait_ge(log_done, n + 1)
                act.activation(rstd[:, :], rstd[:, :], ACT.Exp, scale=-0.5).then_inc(rstd_ready, 1)

            def squares_and_rstds_of_end(end, b, n):
                for half in range(2):
                    for k in range(CT):
                        act.wait_ge(centred_tiles, CT * (2 * end + half) + k + 1)
                        act.activation(end_square(half, k), line(b, half, k), ACT.Square).then_inc(squared_tiles, 1)
                for half in range(2):
                    act.wait_ge(var_ready, n + half + 1)
                    act.activation(end_rstd[half], end_var[half][:, :], ACT.Ln, bias=eps).then_inc(log_done, 1)
                    act.wait_ge(log_done, n + half + 1)
                    act.activation(end_rstd[half], end_rstd[half], ACT.Exp, scale=-0.5).then_inc(rstd_ready, 1)

            def silu_z(i, half):
                for c in range(CT):
                    j = z_item(0, half, c)
                    act.wait_ge(ring_ready, z_item(i, half, c) + 1)
                    after(act, gated, CT * (2 * i + half - 2) + c + 1)
                    act.activation(gate[:, half, c, :], ring[:, j % 2, :], ACT.Silu).then_inc(ring_read, 1)

            def group_rstds(i):
                act.wait_ge(group_var_ready, i + 1)
                act.activation(spread[:, :], group_ps, ACT.Ln, bias=t.gn_eps[0:MP, :]).then_inc(group_log, 1)
                act.wait_ge(group_log, i + 1)
                act.activation(group_rstd[:, :], spread[:, :], ACT.Exp, scale=-0.5).then_inc(group_rstd_ready, 1)

            def pad_image(i):
                for c in range(CT):
                    for half in range(2):
                        j = pad_item(0, c, half)
                        act.wait_ge(ring_ready, pad_item(i, c, half) + 1)
                        if c == TEN:
                            after(act, conv_ready, 2 * i)
                        else:
                            after(act, taps_done[c], len(TAPS) * i)
                        act.activation(pad[c][:, 1 + half * ROWS:1 + (half + 1) * ROWS, 1:1 + WW],
                                       ring[:, j % 2, :].rearrange("p (h w) -> p h w", w=WW), ACT.Identity,
                                       bias=t.b_in1[:, c:c + 1]).then_inc(ring_read, 1)
                    if c != TEN:
                        first_tap(i, c)

            def first_tap(i, c):
                act.wait_ge(ring_read, pad_item(i, c, 1) + 1)
                carry_waits_act()
                act.activation(y[:, i, c, :, :], pad[c][:, 0:HH, 0:WW], ACT.Copy, scale=t.conv_w1[:, c, 0:1]).then_inc(taps_done[c], 1)

            def finish_conv(i, half):
                act.wait_ge(conv_ready, 2 * i + half + 1)
                after(act, ema_steps[1], (2 * CT + 1) * i - CT - 1)
                act.activation(y[:, i, TEN, rows(half), :], conv_ps[:, half, :, :], ACT.Copy).then_inc(conv_read, 1)
                act.activation(turned[:, TEN, :, rows(half)].rearrange("p w h -> p h w"), conv_ps[:, half, :, :], ACT.Copy
                               ).then_inc(conv_read, 1)

            def exchange(i, c):
                act.wait_ge(taps_done[c], len(TAPS) * (i + 1))
                after(act, ema_steps[1], (2 * CT + 1) * i - CT - 1)
                carry_waits_act()
                act.activation(turned[:, c, :, :].rearrange("p w h -> p h w"), y[:, i, c, :, :], ACT.Copy
                               ).then_inc(turned_ready, 1)

            def gate_part(j):
                for half in range(2):
                    load_tables(SILU)
                    squares(j, half, gate_n(j, half))
                    silu_z(j, half)
                    load_tables(EXP_AND_LN)
                    reciprocal_std(gate_n(j, half))

            def first_turn():
                load_tables(EXP_AND_LN)
                squares_and_rstds_of_end(0, 0, gate_n(0, 0))
                load_tables(SILU)
                for half in range(2):
                    silu_z(0, half)
                load_tables(EXP_AND_LN)
                for half in range(2):
                    squares(1, half, gate_n(1, half))
                group_rstds(0)
                for half in range(2):
                    reciprocal_std(gate_n(1, half))
                load_tables(SILU)
                act.wait_ge(borders, CT)
                pad_image(0)
                for half in range(2):
                    silu_z(1, half)
                load_tables(EXP_AND_LN)
                finish_conv(0, 0)
                exchange(0, 0)
                group_rstds(1)
                finish_conv(0, 1)
                exchange(0, 1)

            def turn(i):
                gate_part(i + 1)
                pad_image(i)
                squares(i - 1, 0, final_n(i - 1, 0))
                finish_conv(i, 0)
                squares(i - 1, 1, final_n(i - 1, 1))
                reciprocal_std(final_n(i - 1, 0))
                exchange(i, 0)
                finish_conv(i, 1)
                reciprocal_std(final_n(i - 1, 1))
                exchange(i, 1)
                group_rstds(i + 1)

            def last_turn():
                i = NB - 1
                pad_image(i)
                squares(i - 1, 0, final_n(i - 1, 0))
                finish_conv(i, 0)
                squares(i - 1, 1, final_n(i - 1, 1))
                reciprocal_std(final_n(i - 1, 0))
                exchange(i, 0)
                finish_conv(i, 1)
                reciprocal_std(final_n(i - 1, 1))
                exchange(i, 1)
                squares_and_rstds_of_end(1, i, final_n(i, 0))

            first_turn()
            with act.Fori(1, NB - 1) as i:
                turn(i)
            last_turn()

        @block.tensor
        def _(pe):
            def mean(n, half):
                pe.wait_ge(sum_y_done, 2 * (n - AHEAD) + 2)
                after(pe, centred, n - AHEAD)
                if isinstance(n, int) and n == AHEAD:
                    pe.wait_ge(log_done, AHEAD)
                pe.matmul(mean_ps[:, :], avg, sum_y[:, half, :], start=True, stop=True).then_inc(mean_ready, 1)

            def variance(n):
                pe.wait_ge(sum_square_done, 2 * (n - AHEAD) + 2)
                after(pe, log_done, n)
                pe.matmul(var_ps[:, :], avg, sum_square[:, :], start=True, stop=True).then_inc(var_ready, 1)

            def mean_of_end(b, half):
                for place, k in enumerate((0, TEN, 1)):
                    if b == NB - 1:
                        pe.wait_ge(mixed_columns[k], NB)
                    last = pe.matmul(end_mean[half], avg, part(b, half, k), start=(place == 0), stop=(place == CT - 1))
                last.then_inc(mean_ready, 1)

            def variance_of_end(end, half):
                for k in range(CT):
                    pe.wait_ge(squared_tiles, CT * (2 * end + half) + k + 1)
                    last = pe.matmul(end_var[half][:, :], avg, end_square(half, k), start=(k == 0), stop=(k == CT - 1))
                last.then_inc(var_ready, 1)

            def z(i, half, tiles):
                after(pe, xz_ready, MT * i)
                for c in tiles:
                    j = z_item(0, half, c)
                    after(pe, ring_read, z_item(i, half, c) - 1)
                    for k in range(MT):
                        last = pe.matmul(ring[:, j % 2, :], t.w_in0[:, k, DI + c * P:DI + (c + 1) * P], xz[:, k, cols(half)],
                                         start=(k == 0), stop=(k == MT - 1))
                    last.then_inc(ring_ready, 1)

            def project(b, half, n, w):
                after(pe, out_read, 2 * n)
                for m in range(MT):
                    for k in range(CT):
                        last = pe.matmul(out_ps[:, m, :], w[:, k, m * MP:(m + 1) * MP], part(b, half, k),
                                         start=(k == 0), stop=(k == CT - 1))
                last.then_inc(projected, 1)

            def project_gate(i, half):
                pe.wait_ge(gated, CT * (2 * i + half + 1))
                project(i, half, gate_n(i, half), t.w_out0)

            def project_final(b, half, n):
                pe.wait_ge(scaled, CT * (n + 1))
                project(b, half, n, t.w_out1)

            def group_means(i):
                pe.wait_ge(channel_done, MT * (i + 1))
                after(pe, conv_read, 4 * i - 2)
                pe.matmul(group_ps, t.group_avg, channel[:, :, 0], start=True, stop=True).then_inc(group_mean_ready, 1)

            def group_variances(i):
                pe.wait_ge(group_steps, 4 * i + 4)
                pe.matmul(group_ps, t.group_avg, spread[:, :], start=True, stop=True).then_inc(group_var_ready, 1)

            def project_local(i, c):
                pe.wait_ge(xn_ready, MT * (i + 1))
                for half in range(2):
                    j = pad_item(0, c, half)
                    after(pe, ring_read, pad_item(i, c, half) - 1)
                    for k in range(MT):
                        last = pe.matmul(ring[:, j % 2, :], t.w_in1[:, k, c * P:(c + 1) * P], xn[:, k, cols(half)],
                                         start=(k == 0), stop=(k == MT - 1))
                    last.then_inc(ring_ready, 1)

            def convolve(i, half, taps):
                if taps.start == 0:
                    pe.wait_ge(ring_read, pad_item(i, TEN, 1) + 1)
                    pe.wait_ge(group_log, i + 1)
                    after(pe, conv_read, 4 * i)
                for k in taps:
                    di, dj = TAPS[k]
                    last = pe.matmul(conv_ps[:, half, :, :], diag[:, k, :],
                                     pad[TEN][:, half * ROWS + di:(half + 1) * ROWS + di, dj:dj + WW],
                                     start=(k == 0), stop=(k == len(TAPS) - 1))
                if taps.stop == len(TAPS):
                    last.then_inc(conv_ready, 1)

            def shift_of_beta():
                for m in range(MT):
                    for k in range(CT):
                        last = pe.matmul(out_ps[:, m, 0:1], t.w_out1[:, k, m * MP:(m + 1) * MP], t.beta1[:, k:k + 1],
                                         start=(k == 0), stop=(k == CT - 1))
                last.then_inc(shift_product, 1)

            def norm_and_z(j):
                mean(gate_n(j, 0), 0)
                z(j, 0, (0,))
                mean(gate_n(j, 1), 1)
                z(j, 0, (1, 2))
                variance(gate_n(j, 0))
                z(j, 1, range(CT))
                variance(gate_n(j, 1))

            def first_turn():
                for half in range(2):
                    mean_of_end(0, half)
                z(0, 0, (0,))
                variance_of_end(0, 0)
                variance_of_end(0, 1)
                z(0, 0, (1, 2))
                z(0, 1, range(CT))
                shift_of_beta()
                pe.wait_ge(shift_ready, 1)
                for half in range(2):
                    mean(gate_n(1, half), half)
                    project_gate(0, half)
                variance(gate_n(1, 0))
                group_means(0)
                group_variances(0)
                variance(gate_n(1, 1))
                for c in range(CT):
                    project_local(0, c)
                for half in range(2):
                    z(1, half, range(CT))
                project_gate(1, 0)
                pe.wait_ge(diags, len(TAPS))
                convolve(0, 0, range(0, 4))
                project_gate(1, 1)
                convolve(0, 0, range(4, 9))
                convolve(0, 1, range(0, 4))
                group_means(1)
                convolve(0, 1, range(4, 6))
                group_variances(1)
                convolve(0, 1, range(6, 9))

            def turn(i):
                j, b = i + 1, i - 1
                norm_and_z(j)
                for c in VEC:
                    project_local(i, c)
                project_gate(j, 0)
                project_local(i, TEN)
                project_gate(j, 1)
                convolve(i, 0, range(0, 6))
                mean(final_n(b, 0), 0)
                convolve(i, 0, range(6, 9))
                mean(final_n(b, 1), 1)
                convolve(i, 1, range(0, 2))
                convolve(i, 1, range(2, 5))
                variance(final_n(b, 0))
                convolve(i, 1, range(5, 9))
                variance(final_n(b, 1))
                project_final(b, 0, final_n(b, 0))
                group_means(j)
                project_final(b, 1, final_n(b, 1))
                group_variances(j)

            def last_turn():
                i, b = NB - 1, NB - 2
                for c in range(CT):
                    project_local(i, c)
                convolve(i, 0, range(0, 6))
                mean(final_n(b, 0), 0)
                convolve(i, 0, range(6, 9))
                mean(final_n(b, 1), 1)
                convolve(i, 1, range(0, 2))
                convolve(i, 1, range(2, 5))
                variance(final_n(b, 0))
                convolve(i, 1, range(5, 9))
                variance(final_n(b, 1))
                for half in range(2):
                    project_final(b, half, final_n(b, half))
                pe.wait_ge(conv_read, 4 * NB)
                for half in range(2):
                    mean_of_end(i, half)
                pe.wait_ge(centred, final_n(i, 0) - AHEAD)
                pe.wait_ge(log_done, final_n(i, 0))
                for half in range(2):
                    variance_of_end(1, half)
                pe.wait_ge(out_read, 2 * final_n(i, 0))
                pe.wait_ge(centred_tiles, 4 * CT)
                for half in range(2):
                    for k in range(CT):
                        pe.wait_ge(scaled, CT * final_n(i, half) + k + 1)
                        for m in range(MT):
                            last = pe.matmul(last_out[half][:, m, :], t.w_out1[:, k, m * MP:(m + 1) * MP], part(i, half, k),
                                             start=(k == 0), stop=(k == CT - 1))
                    last.then_inc(projected, 1)

            first_turn()
            with pe.Fori(1, NB - 1) as i:
                turn(i)
            last_turn()

        @block.vector
        def _(dve):
            def normalise_for_z(b):
                after(dve, ring_ready, turn_item(b - 1))
                for k in range(MT):
                    dve.tensor_scalar(xz[:, k, :], x[:, k, b, :], t.gn_mean[:, k, bass.ds(b, 1)], t.gn_rstd[:, k, bass.ds(b, 1)],
                                      ALU.subtract, ALU.mult).then_inc(xz_ready, 1)

            def centre(b, half, n):
                dve.wait_ge(mean_ready, n + 1)
                dve.tensor_tensor(lines(b, half), lines(b, half), mean_ps[:, None, :].broadcast_to([P, CT, NX]), ALU.subtract
                                  ).then_inc(centred, 1)

            def centre_end(b, half, n):
                dve.wait_ge(mean_ready, n + 1)
                for k in range(CT):
                    here = line(b, half, k)
                    dve.tensor_tensor(here, here, end_mean[half], ALU.subtract).then_inc(centred_tiles, 1)

            def scale(b, half, n, gamma, factors=rstd[:, :]):
                dve.wait_ge(rstd_ready, n + 1)
                for k in range(CT):
                    here = line(b, half, k)
                    dve.scalar_tensor_tensor(here, here, gamma[:, k:k + 1], factors, ALU.mult, ALU.mult).then_inc(scaled, 1)

            def centre_gate(j, half):
                centre(j, half, gate_n(j, half))

            def centre_final(b, half):
                centre(b, half, final_n(b, half))

            def scale_final(b, half):
                scale(b, half, final_n(b, half), t.gamma1)

            def scale_gate(j, half):
                scale(j, half, gate_n(j, half), t.gamma0)

            def apply_gate(j, half):
                n = gate_n(j, half)
                for k in range(CT):
                    here = line(j, half, k)
                    dve.wait_ge(ring_read, z_item(j, half, k) + 1)
                    dve.wait_ge(scaled, CT * n + k + 1)
                    dve.scalar_tensor_tensor(here, here, t.beta0[:, k:k + 1], gate[:, half, k, :], ALU.add, ALU.mult).then_inc(gated, 1)

            def residual_gate(j, half):
                n = gate_n(j, half)
                here = x[:, :, j, cols(half)]
                dve.wait_ge(projected, n + 1)
                dve.tensor_tensor(here, out_ps[:, :, :], here, ALU.add).then_inc(out_read, 2)
                dve.wait_ge(out_read, 2 * n + 2)
                carry_waits_dve()
                for k in range(MT):
                    dve.bn_stats(stats[:, k, half, :], x[:, k, j, cols(half)]).then_inc(stats_done, 1)
                if half:
                    dve.wait_ge(stats_done, 2 * MT * (j + 1))
                    carry_waits_dve()
                    for k in range(MT):
                        dve.bn_aggr(channel[:, k, :], stats[:, k, :, :]).then_inc(channel_done, 1)

            def residual_final(b, half, product=out_ps):
                dve.wait_ge(projected, final_n(b, half) + 1)
                for m in range(MT):
                    here = x[:, m, b, cols(half)]
                    dve.scalar_tensor_tensor(here, product[:, m, :], shift[:, m:m + 1], here, ALU.add, ALU.add).then_inc(out_read, 1)

            def group_spread(i):
                dve.wait_ge(group_mean_ready, i + 1)
                dve.tensor_copy(group_mean[:, :], group_ps).then_inc(group_steps, 1)
                dve.wait_ge(group_steps, 4 * i + 1)
                dve.tensor_tensor(spread[:, :], channel[:, :, 0], group_mean[:, :], ALU.subtract).then_inc(group_steps, 1)
                dve.wait_ge(group_steps, 4 * i + 2)
                dve.tensor_tensor(spread[:, :], spread[:, :], spread[:, :], ALU.mult).then_inc(group_steps, 1)
                dve.wait_ge(group_steps, 4 * i + 3)
                dve.tensor_tensor(spread[:, :], spread[:, :], channel[:, :, 1], ALU.add).then_inc(group_steps, 1)

            def normalise_for_local(i):
                dve.wait_ge(group_rstd_ready, i + 1)
                after(dve, ring_ready, turn_item(i))
                for k in range(MT):
                    dve.tensor_scalar(xn[:, k, :], x[:, k, i, :], group_mean[:, k:k + 1], group_rstd[:, k:k + 1],
                                      ALU.subtract, ALU.mult).then_inc(xn_ready, 1)

            def convolve(i, c, taps):
                for k in taps:
                    di, dj = TAPS[k]
                    window, here = pad[c][:, di:di + HH, dj:dj + WW], y[:, i, c, :, :]
                    dve.wait_ge(taps_done[c], len(TAPS) * i + k)
                    dve.scalar_tensor_tensor(here, window, t.conv_w1[:, c, k:k + 1], here, ALU.mult, ALU.add
                                             ).then_inc(taps_done[c], 1)

            zeros_first = factor.rearrange("p l i -> p (l i)")

            def ema_forward(b, axis):
                if axis == 0:
                    dve.wait_ge(conv_read, 4 * (b + 1))
                    for c in VEC:
                        dve.wait_ge(taps_done[c], len(TAPS) * (b + 1))
                else:
                    dve.wait_ge(turned_ready, len(VEC) * (b + 1))
                    for k in range(CT):
                        after(dve, mixed_columns[k], b)
                for k in range(CT):
                    source = y[:, b, k, :, :] if axis == 0 else turned[:, k, :, :]
                    dve.tensor_tensor_scan(ema[axis][:, k, :, :].rearrange("p l i -> p (l i)"), zeros_first,
                                           source.rearrange("p l i -> p (l i)"), 0.0, ALU.mult, ALU.add).then_inc(ema_steps[axis], 1)

            def ema_backward(b, axis):
                done = (2 * CT + 1) * b + CT
                dve.wait_ge(ema_steps[axis], done)
                last = ema[axis][:, :, :, WW - 1]
                dve.tensor_scalar(last, last, 1 / (1 - DECAY ** 2), None, ALU.mult).then_inc(ema_steps[axis], 1)
                dve.wait_ge(ema_steps[axis], done + 1)
                for k in range(CT):
                    line_back = ema[axis][:, k, :, :].rearrange("p l i -> p (l i)")[:, ::-1]
                    dve.tensor_tensor_scan(line_back, zeros_first, line_back, 0.0, ALU.mult, ALU.add).then_inc(ema_steps[axis], 1)

            def mix_rows(b):
                dve.wait_ge(ema_steps[0], (2 * CT + 1) * (b + 1))
                here = y[:, b, :, :, :].rearrange("p k h w -> p (k h w)")
                dve.scalar_tensor_tensor(here, here, MIX_X, ema[0][:, :, :, :].rearrange("p k h w -> p (k h w)"), ALU.mult, ALU.add
                                         ).then_inc(mixed_rows, 1)

            def first_turn():
                for half in range(2):
                    centre_end(0, half, gate_n(0, half))
                dve.memset(factor, DECAY).then_inc(factors, 1)
                dve.wait_ge(factors, 1)
                dve.memset(factor[:, :, 0], 0.0).then_inc(factors, 1)
                for half in range(2):
                    scale(0, half, gate_n(0, half), t.gamma0, end_rstd[half])
                for half in range(2):
                    apply_gate(0, half)
                dve.wait_ge(shift_product, 1)
                dve.tensor_tensor(shift[:, :], out_ps[:, :, 0], t.b_out1, ALU.add).then_inc(shift_ready, 1)
                dve.wait_ge(sems.x_again[0], 16)
                for half in range(2):
                    centre_gate(1, half)
                    residual_gate(0, half)
                group_spread(0)
                normalise_for_local(0)
                scale_gate(1, 0)
                dve.wait_ge(sems.x_again[1], 16)
                normalise_for_z(1)
                scale_gate(1, 1)
                convolve(0, 0, range(1, 9))
                apply_gate(1, 0)
                apply_gate(1, 1)
                convolve(0, 1, range(1, 3))
                residual_gate(1, 0)
                convolve(0, 1, range(3, 6))
                residual_gate(1, 1)
                convolve(0, 1, range(6, 9))
                group_spread(1)

            def turn(i):
                j, b = i + 1, i - 1
                normalise_for_z(j)
                centre_gate(j, 0)
                normalise_for_local(i)
                ema_forward(b, 0)
                centre_gate(j, 1)
                ema_forward(b, 1)
                ema_backward(b, 0)
                scale_gate(j, 0)
                apply_gate(j, 0)
                ema_backward(b, 1)
                scale_gate(j, 1)
                apply_gate(j, 1)
                mix_rows(b)
                residual_gate(j, 0)
                for c in VEC:
                    mix_columns(dve, b, c)
                convolve(i, 0, range(1, 5))
                residual_gate(j, 1)
                centre_final(b, 0)
                convolve(i, 0, range(5, 8))
                centre_final(b, 1)
                convolve(i, 0, range(8, 9))
                convolve(i, 1, range(1, 2))
                scale_final(b, 0)
                convolve(i, 1, range(2, 5))
                scale_final(b, 1)
                residual_final(b, 0)
                group_spread(j)
                convolve(i, 1, range(5, 9))
                residual_final(b, 1)

            def last_turn():
                i, b = NB - 1, NB - 2
                normalise_for_local(i)
                for axis in range(2):
                    ema_forward(b, axis)
                for axis in range(2):
                    ema_backward(b, axis)
                mix_rows(b)
                for c in VEC:
                    mix_columns(dve, b, c)
                convolve(i, 0, range(1, 5))
                centre_final(b, 0)
                convolve(i, 0, range(5, 7))
                centre_final(b, 1)
                convolve(i, 0, range(7, 9))
                convolve(i, 1, range(1, 3))
                scale_final(b, 0)
                convolve(i, 1, range(3, 6))
                scale_final(b, 1)
                residual_final(b, 0)
                convolve(i, 1, range(6, 9))
                for axis in range(2):
                    ema_forward(i, axis)
                residual_final(b, 1)
                for axis in range(2):
                    ema_backward(i, axis)
                mix_rows(i)
                for c in VEC:
                    mix_columns(dve, i, c)
                for half in range(2):
                    centre_end(i, half, final_n(i, half))
                for half in range(2):
                    scale(i, half, final_n(i, half), t.gamma1, end_rstd[half])
                for half in range(2):
                    residual_final(i, half, last_out[half])

            first_turn()
            for b in range(2, NB):
                dve.wait_ge(sems.x_again[b], 16)
            with dve.Fori(1, NB - 1) as i:
                turn(i)
            last_turn()


def build(nc, d, out):
    with ExitStack() as ctx:
        sb = lambda name, shape, dt=F32: ctx.enter_context(nc.sbuf_tensor(name, shape, dt))
        sem = lambda name: ctx.enter_context(nc.semaphore(name))
        sems = Names()
        sems.x_in = [sem(f"x_in{b}") for b in range(NB)]
        sems.x_again = [sem(f"x_again{b}") for b in range(NB)]
        sems.params = [sem("inner_loaded"), sem("model_loaded"), sem("w_dt_loaded")]
        sems.fills, sems.out_done = sem("fills"), sem("out_done")
        t = Names()
        t.inner_params = sb("inner_params", [P, sum(INNER.values())])
        t.model_params = sb("model_params", [MP, sum(MODEL.values())])
        t.w_dt = sb("w_dt", [RK, DI])
        t.avg_inner = sb("avg_inner", [P, P])
        t.xz = sb("xz", [MP, MT, PX])
        t.gn_eps, t.half_log_guard = sb("gn_eps", [P, 1]), sb("half_log_guard", [P, 1])
        t.gn_mean, t.gn_rstd = sb("gn_mean", [MP, MT, NB]), sb("gn_rstd", [MP, MT, NB])
        inner, model = unpack(t.inner_params, INNER), unpack(t.model_params, MODEL)
        t.conv_w0, t.conv_w1, t.conv_b0 = inner["conv_w0"], inner["conv_w1"], inner["conv_b0"]
        t.w_x, t.a_log, t.b_dt, t.d_skip = inner["w_x"], inner["a_log"], inner["b_dt"], inner["d_skip"]
        t.w_out0, t.w_out1, t.b_in1, t.ident = inner["w_out0"], inner["w_out1"], inner["b_in1"], inner["ident"]
        t.gamma0, t.beta0, t.gamma1, t.beta1 = inner["gamma0"], inner["beta0"], inner["gamma1"], inner["beta1"]
        t.w_in0, t.w_in1, t.b_out1, t.group_avg = model["w_in0"], model["w_in1"], model["b_out1"], model["group_avg"]
        u = sb("u", [P, NB, CT, HH, WW])
        y = sb("y", [P, NB, CT, HH, WW])
        stages(nc, t, sems, d, out, u, y)


def stages(nc, t, sems, d, out, u, y):
    with nc.sbuf_tensor("xn0", [MP, MT, NB, PX], F32) as xn:
        load_normalise_and_convolve(nc, t, sems, d, xn, u)
    selective_scans(nc, t, u, y)
    gate_mix_and_project(nc, t, sems, d, out, y, u)


_SOURCES = {"conv_w0": "L0_conv_conv_w", "conv_w1": "L1_conv_conv_w", "w_x": "L0_conv_W_x", "a_log": "L0_conv_A_log",
            "w_out0": "L0_conv_W_out", "w_out1": "L1_conv_W_out", "conv_b0": "L0_conv_conv_b", "b_dt": "L0_conv_b_dt",
            "d_skip": "L0_conv_D_param", "gamma0": "L0_conv_gamma", "beta0": "L0_conv_beta", "b_in1": "L1_conv_b_in",
            "gamma1": "L1_conv_ln_g", "beta1": "L1_conv_ln_b", "w_in0": "L0_conv_W_in", "w_in1": "L1_conv_W_in",
            "b_out1": "L1_conv_b_out"}


def kernel(**inputs):
    import numpy as np
    import concourse.bacc as bacc
    from concourse.bass_utils import run_bass_kernel_spmd as run

    nc = bacc.Bacc("TRN2", target_bir_lowering=False, num_devices=1)
    fixed = {"ident": np.eye(P, dtype=np.float32),
             "group_avg": np.kron(np.eye(MP // 6, dtype=np.float32), np.full((6, 6), 1 / 6, np.float32))}

    def pack(columns, rows):
        parts = [fixed[n] if n in fixed else
                 inputs[_SOURCES[n]].reshape(inputs[_SOURCES[n]].shape[0] // rows, rows, -1).transpose(1, 0, 2).reshape(rows, w)
                 for n, w in columns.items()]
        return np.ascontiguousarray(np.concatenate(parts, axis=1))

    arrays = {"x": np.ascontiguousarray(inputs["x"].reshape(NPOS, DM).T), "w_dt": np.ascontiguousarray(inputs["L0_conv_W_dt"]),
              "inner_params": pack(INNER, P), "model_params": pack(MODEL, MP)}
    maps, d = {}, {}
    for name, a in arrays.items():
        maps[f"in_{name}"] = a
        d[name] = nc.dram_tensor(f"in_{name}", a.shape, F32, kind="ExternalInput").ap()
    out = nc.dram_tensor("out", (DM, NPOS), F32, kind="ExternalOutput").ap()
    build(nc, d, out)
    r = run(nc, [maps], core_ids=[0])
    return np.ascontiguousarray(r.results[0]["out"].T).reshape(NB, HH, WW, DM)
```
